# Optimizing a Trainium2 kernel written in Bass

```python
import numpy as np
import jax
import jax.numpy as jnp

def _softmax(x, axis=-1):
    return jax.nn.softmax(x, axis=axis)

def _gelu(x):
    return jax.nn.gelu(x, approximate=True)

def _silu(x):
    return jax.nn.silu(x)

def _sigmoid(x):
    return jax.nn.sigmoid(x)

def _layernorm(x, axis=-1, eps=1e-05):
    m = jnp.mean(x, axis=axis, keepdims=True)
    v = jnp.var(x, axis=axis, keepdims=True)
    return (x - m) / jnp.sqrt(v + eps)

def _scatter_add(tgt, idx, src, axis=0):
    return tgt.at[idx].add(src)

def _segment_sum(src, seg, n):
    return jax.ops.segment_sum(src, seg, n)
kernel_name = 'mk_flamingo_gated_d1_seqx_r4_fba102'

def setup_inputs(seed: int=0):
    np.random.seed(seed)
    _w = jnp.asarray

    def _rec_inputs():
        import jax
        import jax.numpy as jnp
        _rk = jax.random.key(seed)
        x = 7.22e-05 + 1 * jax.random.normal(jax.random.fold_in(_rk, 1), (2, 1024, 256), jnp.float32)
        _lenS = 1024 - jax.random.randint(jax.random.fold_in(_rk, 7), (2,), 0, max(1, 1024 // 4) + 1, jnp.int32)
        _lenS2 = 77 - jax.random.randint(jax.random.fold_in(_rk, 8), (2,), 0, max(1, 77 // 4) + 1, jnp.int32)
        _ctx_1024P = jax.random.normal(jax.random.fold_in(_rk, 11), (2, 16, 256), jnp.float32)
        _ctx_1024c = jax.random.dirichlet(jax.random.fold_in(_rk, 511), 0.3 * jnp.ones((16,), jnp.float32), (2, 77))
        _ctx_1024t = jnp.einsum('bsk,bkd->bsd', _ctx_1024c, _ctx_1024P)
        _ctx_1024t = _ctx_1024t * jax.lax.rsqrt(jnp.mean(jnp.square(_ctx_1024t)) + 1e-12) * 0.953939
        ctx_1024 = 4.13588e-05 + 0.999923 * (_ctx_1024t + 0.3 * jax.random.normal(jax.random.fold_in(_rk, 611), (2, 77, 256), jnp.float32))
        _validS = jnp.arange(1024)[None, :] < _lenS[:, None]
        _validS2 = jnp.arange(77)[None, :] < _lenS2[:, None]
        _causal = jnp.tril(jnp.ones((1024, 1024), dtype=bool))
        mask_BxS2_ik0 = jnp.where(jnp.broadcast_to(_validS2[:, :], (2, 77)), 0, 1).astype(jnp.int32)
        _g = jax.random.normal(jax.random.fold_in(_rk, 9001), (2, 1), jnp.float32)
        _g = jnp.sign(_g) * jnp.maximum(jnp.abs(_g), 1.0) + (_g == 0) * 1.0
        g_xattn = _g[0]
        g_ffn = _g[1]
        return (x, ctx_1024, mask_BxS2_ik0, g_xattn, g_ffn)
    x, ctx_1024, mask_BxS2_ik0, g_xattn, g_ffn = _rec_inputs()

    def _L0_xattn_setup():
        import jax, jax.numpy as jnp
        import numpy as np
        B, LQ, LK, D = (4, 512, 512, 256)
        H = 16
        HD = D // H

        def _split_heads(x):
            b, l, _ = x.shape
            return x.reshape(b, l, H, HD).transpose(0, 2, 1, 3)
        key = jax.random.key(seed)
        ks = jax.random.split(key, 10)
        s = 0.02
        return {'hidden_states': jax.random.normal(ks[0], (B, LQ, D), jnp.float32), 'context': jax.random.normal(ks[1], (B, LK, D), jnp.float32), 'attention_mask': jax.random.randint(ks[2], (B, LK), 0, 2, jnp.int32), 'q_w': jax.random.normal(ks[3], (D, D), jnp.float32) * s, 'q_b': jnp.zeros((D,), jnp.float32), 'k_w': jax.random.normal(ks[4], (D, D), jnp.float32) * s, 'k_b': jnp.zeros((D,), jnp.float32), 'v_w': jax.random.normal(ks[5], (D, D), jnp.float32) * s, 'v_b': jnp.zeros((D,), jnp.float32)}
    _L0_xattn_all = _L0_xattn_setup()
    _L0_xattn_in = {k: v for k, v in _L0_xattn_all.items() if k in ('q_w', 'q_b', 'k_w', 'k_b', 'v_w', 'v_b')}
    del _L0_xattn_all

    def _L0_ffn_setup():
        import jax, jax.numpy as jnp
        import numpy as np
        TOP_K = 2
        key = jax.random.key(seed)
        k1, k2, k3, k4 = jax.random.split(key, 4)
        B, N, D, E, F = (4, 512, 256, 8, 1024)
        x = jax.random.normal(k1, (B, N, D), dtype=jnp.float32)
        gate_w = jax.random.normal(k2, (D, E), dtype=jnp.float32) * D ** (-0.5)
        w1 = jax.random.normal(k3, (E, D, F), dtype=jnp.float32) * D ** (-0.5)
        w2 = jax.random.normal(k4, (E, F, D), dtype=jnp.float32) * F ** (-0.5)
        return {'x': x, 'gate_w': gate_w, 'w1': w1, 'w2': w2}
    _L0_ffn_all = _L0_ffn_setup()
    _L0_ffn_in = {k: v for k, v in _L0_ffn_all.items() if k in ('gate_w', 'w1', 'w2')}
    del _L0_ffn_all
    return {'x': x, 'ctx_1024': ctx_1024, 'mask_BxS2_ik0': mask_BxS2_ik0, 'g_xattn': g_xattn, 'g_ffn': g_ffn, 'L0_xattn_q_w': _L0_xattn_in['q_w'], 'L0_xattn_q_b': _L0_xattn_in['q_b'], 'L0_xattn_k_w': _L0_xattn_in['k_w'], 'L0_xattn_k_b': _L0_xattn_in['k_b'], 'L0_xattn_v_w': _L0_xattn_in['v_w'], 'L0_xattn_v_b': _L0_xattn_in['v_b'], 'L0_ffn_gate_w': _L0_ffn_in['gate_w'], 'L0_ffn_w1': _L0_ffn_in['w1'], 'L0_ffn_w2': _L0_ffn_in['w2']}

def reference(x, ctx_1024, mask_BxS2_ik0, g_xattn, g_ffn, L0_xattn_q_w, L0_xattn_q_b, L0_xattn_k_w, L0_xattn_k_b, L0_xattn_v_w, L0_xattn_v_b, L0_ffn_gate_w, L0_ffn_w1, L0_ffn_w2):
    import jax
    import jax.numpy as jnp

    def _L0_xattn_ref(hidden_states, context, attention_mask, q_w, q_b, k_w, k_b, v_w, v_b):
        import jax, jax.numpy as jnp
        import numpy as np
        B, LQ, LK, D = (4, 512, 512, 256)
        H = 16
        HD = D // H

        def _split_heads(x):
            b, l, _ = x.shape
            return x.reshape(b, l, H, HD).transpose(0, 2, 1, 3)
        q = _split_heads(hidden_states @ q_w.T + q_b)
        k = _split_heads(context @ k_w.T + k_b)
        v = _split_heads(context @ v_w.T + v_b)
        scores = jnp.einsum('bhqd,bhkd->bhqk', q, k) / jnp.sqrt(jnp.float32(HD))
        mask = (attention_mask > 0)[:, None, None, :]
        scores = jnp.where(mask, -jnp.inf, scores)
        probs = jax.nn.softmax(scores, axis=-1)
        ctx = jnp.einsum('bhqk,bhkd->bhqd', probs, v)
        ctx = ctx.transpose(0, 2, 1, 3).reshape(ctx.shape[0], ctx.shape[2], H * HD)
        return ctx

    def _L0_ffn_ref(x, gate_w, w1, w2):
        import jax, jax.numpy as jnp
        import numpy as np
        TOP_K = 2
        E = gate_w.shape[-1]
        gate_logits = jnp.einsum('bnd,de->bne', x, gate_w)
        gate_probs = jax.nn.softmax(gate_logits, axis=-1)
        top_k_probs, top_k_idx = jax.lax.top_k(gate_probs, TOP_K)
        top_k_weights = top_k_probs / jnp.sum(top_k_probs, axis=-1, keepdims=True)
        comb = jnp.sum(jax.nn.one_hot(top_k_idx, E, dtype=x.dtype) * top_k_weights[..., None], axis=2)
        h = jax.nn.gelu(jnp.einsum('bnd,edf->benf', x, w1))
        expert_out = jnp.einsum('benf,efd->bend', h, w2)
        output = jnp.einsum('bne,bend->bnd', comb, expert_out)
        return output
    x = x + jnp.tanh(g_xattn[0]) * _L0_xattn_ref(_layernorm(x, axis=-1), ctx_1024, mask_BxS2_ik0, L0_xattn_q_w, L0_xattn_q_b, L0_xattn_k_w, L0_xattn_k_b, L0_xattn_v_w, L0_xattn_v_b)
    x = x + jnp.tanh(g_ffn[0]) * _L0_ffn_ref(_layernorm(x, axis=-1), L0_ffn_gate_w, L0_ffn_w1, L0_ffn_w2)
    return x

_drawn_inputs = setup_inputs


def setup_inputs(seed=0):
    import zlib

    import numpy as np

    out = dict(_drawn_inputs(seed))
    spreads = {'L0_xattn_q_b': (0.0, 0.645), 'L0_xattn_k_b': (0.0, 0.8), 'L0_xattn_v_b': (0.0, 0.1)}
    factors = {}
    for name, (base, spread) in spreads.items():
        noise = np.random.default_rng([zlib.crc32(name.encode()), seed]).standard_normal(out[name].shape)
        drawn = base * np.exp(spread * noise) if base else spread * noise
        out[name] = jnp.asarray(drawn.astype(out[name].dtype))
    for name, factor in factors.items():
        out[name] = (out[name] * factor).astype(out[name].dtype)
    return out
```

```python
from contextlib import ExitStack

import concourse.bass as bass
from concourse import mybir

F32 = mybir.dt.float32
F16 = mybir.dt.float16
BF16 = mybir.dt.bfloat16
I32 = mybir.dt.int32
ACT = mybir.ActivationFunctionType
ALU = mybir.AluOpType
AX = mybir.AxisListType

P = 128
MB = 256
EPS = 1e-5
WSCALE = 256.0
QSCALE = 16.0
MASKED = -1.0e30
UNROLL = 4
MU = 2
DEPTH = 3


def at(t, n=1):
    return bass.ds(t, n)


def flamingo_moe_block(nc, x, ctxT, mask, g_xattn, g_ffn, wqT, q_b, wkT, k_b, wvT, v_b, gate_w, w1, w2, out):
    B, L, D = x.shape
    LK = mask.shape[1]
    H, HD = 16, D // 16
    E, _, F = w1.shape
    NT = B * L // P
    TB = L // P
    KD = D // P
    KF = F // P
    HG = P // HD
    NG = H // HG
    GK = HG * LK
    HK = H * LK
    HB = 6
    NC = -(-HK // P)
    TAIL = HK - (NC - 1) * P
    VW = HD + 1
    CH = 3
    head0 = [min(P * c // LK, H - CH) for c in range(NC)]
    PARTS = [(0, 0, 0, 0, 6), (1, 0, 0, 6, 2), (1, 2 * LK, 1, 0, 4), (2, 0, 1, 4, 4)]
    NB = 2 * B * L // MB + E - 1
    MH = MB // P
    QF = 512 // MB
    NQ = KF // QF
    CAP = B * L + MB
    DUMP = (E - 1) * CAP + B * L
    GT = UNROLL
    CONSTS = 11
    WCH = 2 * E * KD

    xs = nc.dram_tensor("token_rows", [E * CAP, 2 * D], F16).ap()
    ys = nc.dram_tensor("expert_out", [NB * MB, D], F32).ap()

    with ExitStack() as ctx:
        def sb(name, shape, dt):
            return ctx.enter_context(nc.sbuf_tensor(name, shape, dt))

        def ps(name, shape, dt=F32):
            return ctx.enter_context(nc.psum_tensor(name, shape, dt))

        def sem(name):
            return ctx.enter_context(nc.semaphore(name))

        X = sb("X", [P, NT, D], F32)
        W1 = sb("W1", [P, E, 2, KD, F], F16)
        W2 = sb("W2", [P, E, 2, KF, D], F16)
        stage = sb("stage", [P, 2, F], F32)
        kbd = sb("kbd", [P, B, NG, 2, GK], F16)
        vbd = sb("vbd", [P, B, NC, CH * VW], F32)
        prob = sb("prob", [P, 2, HK], F32)
        probT = sb("probT", [P, NC * P], F32)
        rows = sb("rows", [P, GT, 2 * D], F16)
        xn = sb("xn", [P, 2, D], F32)
        xnT = sb("xnT", [P, 2, 2, KD, P], F16)
        qT = sb("qT", [P, 2, 2, NG, P], F16)
        att = sb("att", [P, D], F32)
        xn2 = sb("xn2", [P, GT, D], F32)
        xn2T = sb("xn2T", [P, 2, D], F32)
        wqs = sb("wqs", [P, 2, KD, D], F16)
        lent = {"probT": [probT[:, :], 0],
                "prob": [prob[:, :, :].rearrange("p a b -> p (a b)"), 0]}

        def setup_view(n, where="probT"):
            room, o = lent[where]
            lent[where][1] = o + n
            assert o + n <= room.shape[1]
            return room[:, o:o + n]

        wk = setup_view(KD * D, "prob").rearrange("p (k n) -> p k n", k=KD)
        wv = setup_view(KD * D, "prob").rearrange("p (k n) -> p k n", k=KD)
        cT = setup_view(KD * B * LK).rearrange("p (k n) -> p k n", k=KD)
        vaug = setup_view(B * H * VW).rearrange("p (b h w) -> p b h w", b=B, h=H)
        spread = setup_view(LK + P)
        maski = setup_view(B * LK)[0:1, :].bitcast(I32).rearrange("p (b k) -> p b k", b=B)
        vb = setup_view(D, "prob")
        wq = setup_view(KD * D, "prob").rearrange("p (k n) -> p k n", k=KD)
        kTf = setup_view(NG * B * LK, "prob").rearrange("p (g n) -> p g n", g=NG)
        kTs = setup_view(NG * B * LK, "prob").bitcast(F16).rearrange("p (s g n) -> p s g n", s=2, g=NG)
        lent["stage"] = [stage[:, :, :].rearrange("p a n -> p (a n)"), 0]
        over = setup_view(E * NT, "stage").rearrange("p (e k) -> p e k", e=E)
        cum = setup_view(E * E, "stage").rearrange("p (e k) -> p e k", e=E)
        cd = setup_view(2 * NT * E, "stage").rearrange("p (c t e) -> p c t e", c=2, t=NT)
        past = setup_view(NB * E, "stage")[0:1, :].rearrange("p (j e) -> p j e", j=NB)
        pastc = setup_view(NB * E, "stage")[0:1, :].rearrange("p (j e) -> p j e", j=NB)
        zrows = setup_view(MH * D, "stage").bitcast(F16).rearrange("p (h d) -> p h d", h=MH)
        cdr = setup_view(2 * NT, "stage").rearrange("p (c t) -> p c t", c=2)
        cslot = setup_view(2 * NT, "stage").rearrange("p (c t) -> p c t", c=2)
        upto = setup_view(E * E, "stage").rearrange("p (e k) -> p e k", e=E)
        bexp = setup_view(NB, "stage")[0:1, :]
        brow = setup_view(2 * NB, "stage")[0:1, :].rearrange("p (s j) -> p s j", s=2)
        hid = lent["prob"][0][:, 0:NQ * 512].rearrange("p (q n) -> p q n", q=NQ)
        hidS = kbd[:, :, :, :, :].rearrange("p b g s n -> p (b g s n)")[:, 0:NQ * 2 * 512].rearrange(
            "p (q s n) -> p q s n", q=NQ, s=2)
        xb = rows[:, :, :].rearrange("p (a h) d -> p a h d", a=2)
        xbT = probT[:, 0:2 * D * MH].bitcast(F16).rearrange("p (a s k n) -> p a s k n", a=2, s=2, k=KD)
        yb = xn2[:, :, :].rearrange("p (a h) d -> p a h d", a=2)
        picks = stage[:, :, :].rearrange("p a (t c d) -> p (a t) c d", c=2, d=D)
        gate = sb("gate", [P, KD, E], F32)
        ident = sb("ident", [P, P], F32)
        wscale = sb("wscale", [P, 1], F32)
        ident16 = sb("ident16", [P, P], F16)
        before = sb("before", [P, P], BF16)
        ones = sb("ones", [P, P], BF16)
        headm = sb("headm", [P, HG, 1], F32)
        chunkm = sb("chunkm", [P, NC, CH], F32)
        maskrow = sb("maskrow", [1, B, 1, LK], BF16)
        qb = sb("qb", [P, NG], F32)
        qb16 = sb("qb16", [P, NG], F32)
        kb = sb("kb", [P, NG], F32)
        gains = sb("gains", [P, 4], F32)
        gffn = sb("gffn", [P, 1], F32)
        iota_i = xn2[:, :, :].rearrange("p a d -> p (a d)")[:, 0:2 * NB].bitcast(I32).rearrange("p (s j) -> p s j", s=2)
        stat1 = xn2T[:, :, :].rearrange("p a d -> p (a d)")[:, 0:NT * 6].rearrange("p (t s) -> p t s", t=NT)
        mv1 = sb("mv1", [P, NT, 2], F32)
        ve1 = sb("ve1", [P, NT], F32)
        rstd1 = sb("rstd1", [P, NT], F32)
        neghalf = sb("neghalf", [P, NT], F32)
        mx = sb("mx", [P, 2, H], F32)
        rsum = sb("rsum", [P, 2, H], F32)
        stat2 = sb("stat2", [P, 2, 6], F32)
        mv2 = sb("mv2", [P, 2, 2], F32)
        ve2 = sb("ve2", [P, 2, 1], F32)
        rstd2 = sb("rstd2", [P, 2, 1], F32)
        logit = sb("logit", [P, NT, E], F32)
        rt = {n: sb("rt_" + n, [P, GT, E], F32) for n in
              ("shift", "exp", "p", "eq", "c", "p2", "rank", "s1", "s2")}
        rv = {n: sb("rv_" + n, [P, GT], F32) for n in
              ("max", "sum", "rsum", "m1", "f1", "m2", "f2", "ws", "rws")}
        chosen = sb("chosen", [P, 2, NT, E], BF16)
        pick16 = sb("pick16", [P, GT, E], BF16)
        comb = sb("comb", [P, 2, NT], F32)
        slot = sb("slot", [P, 2, NT], F32)
        sloti = sb("sloti", [P, 2, GT], I32)
        count = sb("count", [P, E], F32)
        desc = sb("desc", [P, E], F32)
        eoff = sb("eoff", [P, E], F32)
        kstep = sb("kstep", [P, NT], F32)
        jstep = sb("jstep", [1, NB], F32)
        nblk = sb("nblk", [P, E], F32)
        end = sb("end", [P, E], F32)
        delta = sb("delta", [P, 2, E], F32)
        coef = sb("coef", [1, E], F32)
        blk = sb("blk", [1, 2, NB], I32)
        padrow = sb("padrow", [1, E], F32)
        padi = sb("padi", [1, E], I32)
        csloti = sb("csloti", [P, 2, NT], I32)
        part = xn
        res = qT[:, :, :, :, :].rearrange("p a s g n -> p a (s g n)").bitcast(F32)

        pT = ps("pT", [P, 512])
        pQ = ps("pQ", [P, 512])
        pS = ps("pS", [P, 3, 512])
        pP = ps("pP", [P, 2, 512])
        pO = ps("pO", [P, 512])
        hbank = [pQ, pS[:, 0, :], pS[:, 1, :], pS[:, 2, :]]
        ybank = [pP[:, 0, :], pP[:, 1, :]]
        tbank = [pT[:, :], pO[:, :]]

        x_in = sem("x_in")
        wq_in = sem("wq_in")
        kv_in = sem("kv_in")
        small_in = sem("small_in")
        gate_in = sem("gate_in")
        mask_in = sem("mask_in")
        gains_in = sem("gains_in")
        const_made = sem("const_made")
        ident_made = sem("ident_made")
        chunk_made = sem("chunk_made")
        head_made = sem("head_made")
        tanh_done = sem("tanh_done")
        qb_done = sem("qb_done")
        wq_hi = sem("wq_hi")
        wq_lo = sem("wq_lo")
        k_ps = sem("k_ps")
        k_sb = sem("k_sb")
        kT_hi = sem("kT_hi")
        kT_lo = sem("kT_lo")
        kbd_hi = sem("kbd_hi")
        kbd_done = sem("kbd_done")
        v_ps = sem("v_ps")
        vaug_done = sem("vaug_done")
        vc_ps = sem("vc_ps")
        vbd_done = sem("vbd_done")
        mask_done = sem("mask_done")
        stat1_done = sem("stat1_done")
        mv1_done = sem("mv1_done")
        ve1_done = sem("ve1_done")
        rstd1_done = sem("rstd1_done")
        xn_ready = sem("xn_ready")
        xnT_ps = sem("xnT_ps")
        xnT_hi = sem("xnT_hi")
        xnT_lo = sem("xnT_lo")
        q_ps = sem("q_ps")
        q_hi = sem("q_hi")
        q_lo = sem("q_lo")
        s_ps = sem("s_ps")
        max_done = sem("max_done")
        shift_done = sem("shift_done")
        prob_ready = sem("prob_ready")
        pt_ps = sem("pt_ps")
        pt_sb = sem("pt_sb")
        o_ps = sem("o_ps")
        rsum_done = sem("rsum_done")
        att_done = sem("att_done")
        x1_done = sem("x1_done")
        stat2_done = sem("stat2_done")
        mv2_done = sem("mv2_done")
        ve2_done = sem("ve2_done")
        rstd2_done = sem("rstd2_done")
        xn2_ready = sem("xn2_ready")
        row_hi = sem("row_hi")
        row_lo = sem("row_lo")
        xn2T_ps = sem("xn2T_ps")
        xn2T_sb = sem("xn2T_sb")
        logit_ps = sem("logit_ps")
        logit_sb = sem("logit_sb")
        w_hi = sem("w_hi")
        w_scaled = sem("w_scaled")
        w_lo = sem("w_lo")
        route_done = sem("route_done")
        exp_ready = sem("exp_ready")
        pick_ready = sem("pick_ready")
        rank_ps = sem("rank_ps")
        rank_used = sem("rank_used")
        slots_ready = sem("slots_ready")
        rows_sent = sem("rows_sent")
        zero_made = sem("zero_made")
        dump_sent = sem("dump_sent")
        final_done = sem("final_done")
        blk_ready = sem("blk_ready")
        pads_sent = sem("pads_sent")
        xbT_ps = sem("xbT_ps")
        xbT_sb = sem("xbT_sb")
        h_ps = sem("h_ps")
        h_act = sem("h_act")
        h_hi = sem("h_hi")
        h_lo = sem("h_lo")
        h_used = sem("h_used")
        y_sb = sem("y_sb")
        picked = sem("picked")
        part_done = sem("part_done")
        res_done = sem("res_done")
        w_in = [sem(f"w_in{i}") for i in range(2)]
        xb_in = [sem(f"xb_in{i}") for i in range(2)]
        y_out = [sem(f"y_out{i}") for i in range(2)]
        out_sent = [sem(f"out_sent{i}") for i in range(2)]
        pick_in = [sem(f"pick_in{i}") for i in range(4)]

        def some(count):
            return not isinstance(count, int) or count > 0

        def attention_steps(eng, step):
            for s in range(UNROLL):
                step(s, s, None)
            with eng.Fori(1, NT // UNROLL) as i:
                for u in range(UNROLL):
                    step(i * UNROLL + u, u, i - 1 if u == UNROLL - 1 else None)
            for s in range(NT, NT + UNROLL):
                step(s, s - NT, NT // UNROLL - 1 if s == NT + UNROLL - 1 else None)

        def live(t):
            return not isinstance(t, int) or 0 <= t < NT


        def batch_of(eng, t):
            return t // TB if isinstance(t, int) else eng.snap(t // TB)

        def expert_of(eng, s):
            return s // 2 if isinstance(s, int) else eng.snap(s // 2)

        block = ctx.enter_context(nc.Block())

        @block.sync
        def _(sp):
            xr = x.rearrange("b (t p) d -> p (b t) d", p=P)
            for c in range(4):
                n = NT // 4
                sp.dma_start(X[:, c * n:(c + 1) * n, :], xr[:, c * n:(c + 1) * n, :]).then_inc(x_in, 16)
                sp.wait_ge(x_in, 16 * (c + 1))
                if c == 0:
                    sp.dma_start(wq[:, :, :], wqT.rearrange("(k p) n -> p k n", p=P)).then_inc(wq_in, 16)
                    sp.dma_start(wk, wkT.rearrange("(k p) n -> p k n", p=P)).then_inc(kv_in, 16)
                    sp.dma_start(wv, wvT.rearrange("(k p) n -> p k n", p=P)).then_inc(kv_in, 16)
                    sp.dma_start(cT, ctxT.rearrange("(k p) n -> p k n", p=P)).then_inc(kv_in, 16)
                    sp.dma_start(vb[0:LK, :], v_b.rearrange("(o d) -> o d", o=1).broadcast_to([LK, D])).then_inc(kv_in, 16)
            w1r = w1.rearrange("e (k p) f -> p e k f", p=P)
            w2r = w2.rearrange("e (c f p) d -> p e c f d", p=P, c=2)

            def load_expert(e):
                for c in range(4):
                    if not (isinstance(e, int) and c < 2):
                        if some(e * 4 + c - 1):
                            sp.wait_ge(w_lo, e * 4 + c - 1)
                    if c < 2:
                        src = w1r[:, at(e), c, :].rearrange("p o f -> p (o f)")
                        dst = stage[:, c % 2, :]
                    else:
                        src = w2r[:, at(e), c - 2, :, :].rearrange("p o f d -> p (o f) d")
                        dst = stage[:, c % 2, :].rearrange("p (f d) -> p f d", d=D)
                    sp.dma_start(dst, src).then_inc(w_in[c % 2], 16)

            load_expert(0)
            with sp.Fori(1, E) as e:
                load_expert(e)

            sp.wait_ge(blk_ready, 3)
            sp.wait_ge(dump_sent, 16)
            r = sp.alloc_register("row")
            for e in range(E):
                sp.reg_load(r, padi[0:1, e:e + 1])
                sp.dma_start(xs[at(sp.snap(r, min_val=0, max_val=(E - 1) * CAP + B * L), MB), :].rearrange(
                    "(h p) d -> p h d", p=P), zrows).then_inc(pads_sent, 16)
            sp.wait_ge(pads_sent, 16 * E)
            sp.wait_ge(rows_sent, 16 * 2 * NT)

            def load_block(j, a):
                if some(j - 1):
                    n = sp.snap(j - 1)
                    sp.wait_ge(const_made, CONSTS)
                    sp.wait_ge(xbT_ps, n)
                sp.reg_load(r, blk[0:1, 1, at(j)])
                sp.dma_start(xb[:, a, :, :], xs[at(sp.snap(r, min_val=0, max_val=DUMP), MB), :].rearrange(
                    "(h p) d -> p h d", p=P)).then_inc(xb_in[a], 16)

            def store_block(j, a):
                n = sp.snap(j + 1)
                sp.wait_ge(const_made, CONSTS)
                sp.wait_ge(y_sb, n)
                sp.dma_start(ys[at(j * MB, MB), :].rearrange("(h p) d -> p h d", p=P), yb[:, a, :, :]).then_inc(y_out[a], 16)

            load_block(0, 0)
            load_block(1, 1)
            load_block(2, 0)
            with sp.Fori(0, (NB - 3) // 2) as i:
                for a in range(2):
                    load_block(i * 2 + a + 3, (a + 1) % 2)
                    store_block(i * 2 + a, a)
            for j in range(NB - 3, NB):
                store_block(j, j % 2)

            outr = out.rearrange("b (t p) d -> p (b t) d", p=P)
            with sp.Fori(0, NT // 2) as i:
                for a in range(2):
                    sp.wait_ge(res_done, i * 2 + a + 1)
                    sp.dma_start(outr[:, at(i * 2 + a), :].rearrange("p o d -> p (o d)"),
                                 res[:, a, :]).then_inc(out_sent[a], 16)
            for a in range(2):
                sp.wait_ge(out_sent[a], NT // 2 * 16)

        @block.gpsimd
        def _(pool):
            pool.memset(ident[:, :], 0.0).then_inc(const_made, 1)
            pool.memset(ident16[:, :], 0.0).then_inc(const_made, 1)
            pool.memset(neghalf[:, :], -0.5).then_inc(const_made, 1)
            pool.memset(ones[:, :], 1.0).then_inc(const_made, 1)
            pool.memset(wscale[:, :], WSCALE).then_inc(const_made, 1)
            pool.memset(before[:, :], 1.0).then_inc(const_made, 1)
            pool.memset(headm[:, :, :], 1.0).then_inc(const_made, 1)
            pool.memset(chunkm[:, :, :], 1.0).then_inc(const_made, 1)
            pool.memset(spread[0:LK, :], 0.0).then_inc(const_made, 1)
            pool.memset(vaug[0:LK, :, :, HD:VW], 1.0).then_inc(const_made, 1)
            pool.memset(count[:, :], 0.0).then_inc(const_made, 1)
            pool.wait_ge(const_made, CONSTS)
            for t in (ident, ident16):
                pool.affine_select(out=t[:, :], in_=t[:, :], compare_op=ALU.not_equal, fill=1.0, base=0,
                                   pattern=[[-1, P]], channel_multiplier=1).then_inc(ident_made, 1)
            pool.affine_select(out=headm[:, :, 0], in_=headm[:, :, 0], compare_op=ALU.is_ge, fill=0.0, base=0,
                               pattern=[[-HD, HG]], channel_multiplier=1).then_inc(head_made, 1)
            pool.wait_ge(head_made, 1)
            pool.affine_select(out=headm[:, :, 0], in_=headm[:, :, 0], compare_op=ALU.is_ge, fill=0.0, base=HD - 1,
                               pattern=[[HD, HG]], channel_multiplier=-1).then_inc(head_made, 1)
            for n in range(-(-(LK + P) // LK)):
                pool.affine_select(out=spread[0:LK, :], in_=spread[0:LK, :], compare_op=ALU.not_equal, fill=1.0,
                                   base=n * LK, pattern=[[-1, LK + P]], channel_multiplier=1).then_inc(chunk_made, 1)
                pool.wait_ge(chunk_made, n + 1)
            nsp = -(-(LK + P) // LK)
            for c in range(NC):
                pool.affine_select(out=chunkm[:, c, :], in_=chunkm[:, c, :], compare_op=ALU.is_ge, fill=0.0,
                                   base=c * P - LK * head0[c], pattern=[[-LK, CH]],
                                   channel_multiplier=1).then_inc(chunk_made, 1)
            pool.wait_ge(chunk_made, nsp + NC)
            for c in range(NC):
                pool.affine_select(out=chunkm[:, c, :], in_=chunkm[:, c, :], compare_op=ALU.is_ge, fill=0.0,
                                   base=LK * head0[c] + LK - 1 - c * P, pattern=[[LK, CH]],
                                   channel_multiplier=-1).then_inc(chunk_made, 1)
            pool.affine_select(out=before[:, :], in_=before[:, :], compare_op=ALU.is_gt, fill=0.0, base=0,
                               pattern=[[1, P]], channel_multiplier=-1).then_inc(chunk_made, 1)
            pool.iota(iota_i[:, 0, :], pattern=[[MB, NB]], base=0, channel_multiplier=0).then_inc(chunk_made, 1)
            pool.iota(iota_i[:, 1, :], pattern=[[1, NB]], base=0, channel_multiplier=0).then_inc(chunk_made, 1)
            pool.wait_ge(chunk_made, nsp + 2 * NC + 3)
            pool.tensor_copy(kstep[:, :], iota_i[:, 0, 0:NT]).then_inc(chunk_made, 1)
            pool.tensor_copy(jstep[:, :], iota_i[0:1, 1, :]).then_inc(chunk_made, 1)
            pool.tensor_scalar(desc[:, :], iota_i[:, 1, 0:E], -1.0, float(E), ALU.mult, ALU.add).then_inc(chunk_made, 1)
            pool.tensor_scalar(eoff[:, :], iota_i[:, 1, 0:E], float(CAP), None, ALU.mult).then_inc(chunk_made, 1)

            pool.wait_ge(kT_lo, 1)
            pool.wait_ge(head_made, 2)
            n = 0
            for b in range(B):
                for g in range(NG):
                    for s in range(2):
                        n += 1
                        pool.tensor_tensor(
                            kbd[:, b, g, s, :].rearrange("p (h k) -> p h k", h=HG),
                            kTs[:, s, g, b * LK:(b + 1) * LK].rearrange("p (o k) -> p o k", o=1).broadcast_to([P, HG, LK]),
                            headm[:, :, :].broadcast_to([P, HG, LK]), ALU.mult).then_inc(kbd_done, 1)

            pool.wait_ge(mv1_done, NT)
            pool.tensor_scalar(ve1[:, :], mv1[:, :, 1], EPS, None, ALU.add).then_inc(ve1_done, 1)
            pool.wait_ge(ve1_done, 1)
            pool.tensor_tensor(rstd1[:, :], ve1[:, :], neghalf[:, :], ALU.pow).then_inc(rstd1_done, 1)
            pool.wait_ge(rstd1_done, 1)

            def weight_low(s, u):
                e = expert_of(pool, s)
                for c in range(2):
                    pool.wait_ge(w_hi, s * 2 + c + 1)
                    pool.tensor_tensor(stage[:, c, :], stage[:, c, :], wscale[:, :].broadcast_to([P, F]),
                                       ALU.mult).then_inc(w_scaled, 1)
                    n = pool.snap(s * 2 + c + 1)
                    pool.wait_ge(const_made, CONSTS)
                    pool.wait_ge(w_scaled, n)
                    if u % 2 == 0:
                        hi, lo = [W1[:, at(e), p, c, :].rearrange("p o f -> p (o f)") for p in range(2)]
                    else:
                        hi, lo = [W2[:, at(e), p, c * KF // 2:(c + 1) * KF // 2, :].rearrange(
                            "p o f d -> p (o f d)") for p in range(2)]
                    pool.tensor_tensor(lo, stage[:, c, :], hi, ALU.subtract).then_inc(w_lo, 1)

            def step(s, u, grp):
                t, a = s - 2, u % 2
                if live(t):
                    pool.wait_ge(ve2_done, t + 1)
                    if some(t - 1):
                        pool.wait_ge(xn2_ready, t - 1)
                    pool.tensor_tensor(rstd2[:, a, :], ve2[:, a, :], neghalf[:, 0:1], ALU.pow).then_inc(rstd2_done, 1)
                t, r = s - GT, u
                if live(t):
                    n = pool.snap(t + 1)
                    pool.wait_ge(const_made, CONSTS)
                    pool.wait_ge(xn2_ready, n)
                    pool.tensor_copy(rows[:, r, 0:D], xn2[:, r, :]).then_inc(row_hi, 1)
                    pool.wait_ge(row_hi, t + 1)
                    pool.tensor_tensor(rows[:, r, D:2 * D], xn2[:, r, :], rows[:, r, 0:D],
                                       ALU.subtract).then_inc(row_lo, 1)
                if grp is not None:
                    t0 = s - (2 * UNROLL - 1)
                    n = pool.snap(grp + 1)
                    pool.wait_ge(const_made, CONSTS)
                    pool.wait_ge(slots_ready, n)
                    n = pool.snap(t0 + GT)
                    pool.wait_ge(const_made, CONSTS)
                    pool.wait_ge(row_lo, n)
                    for k in range(GT):
                        for c in range(2):
                            pool.indirect_dma_start(
                                out=xs[:, :], out_offset=bass.IndirectOffsetOnAxis(ap=sloti[:, c, k:k + 1], axis=0),
                                in_=rows[:, k, :], in_offset=None).then_inc(rows_sent, 16)
                if live(s):
                    weight_low(s, u)
                if grp is not None:
                    pool.wait_ge(rows_sent, (t0 + GT) * 32)

            attention_steps(pool, step)

            pool.wait_ge(w_lo, WCH)
            pool.memset(zrows, 0.0).then_inc(zero_made, 1)
            pool.memset(upto[:, :, :], 1.0).then_inc(zero_made, 1)
            pool.wait_ge(zero_made, 2)
            pool.affine_select(out=upto[:, :, :], in_=upto[:, :, :], compare_op=ALU.is_ge, fill=0.0, base=0,
                               pattern=[[1, E], [-1, E]], channel_multiplier=0).then_inc(zero_made, 1)
            pool.dma_start(xs[DUMP:DUMP + MB, :].rearrange("(h p) d -> p h d", p=P), zrows).then_inc(dump_sent, 16)

            pool.wait_ge(final_done, 7)
            pool.wait_ge(pads_sent, 16 * E)
            for a in range(2):
                pool.wait_ge(y_out[a], 16 * ((NB + 1 - a) // 2))

            def gather(t, a):
                for c in range(2):
                    pool.indirect_dma_start(
                        out=picks[:, a, c, :], out_offset=None, in_=ys[:, :],
                        in_offset=bass.IndirectOffsetOnAxis(ap=csloti[:, c, t:t + 1], axis=0)).then_inc(pick_in[a], 16)

            for t in range(NT):
                if some(t - 3):
                    pool.wait_ge(res_done, t - 3)
                gather(t, t % 4)

        @block.scalar
        def _(act):
            act.dma_start(qb[:, :], q_b).then_inc(small_in, 16)
            act.dma_start(kb[:, :], k_b).then_inc(small_in, 16)
            act.dma_start(gains[:, 0:1], g_xattn.rearrange("(o d) -> o d", o=1).broadcast_to([P, 1])).then_inc(gains_in, 16)
            act.dma_start(gains[:, 1:2], g_ffn.rearrange("(o d) -> o d", o=1).broadcast_to([P, 1])).then_inc(gains_in, 16)
            act.dma_start(maski[:, :, :], mask.rearrange("(o b) k -> o b k", o=1)).then_inc(mask_in, 16)
            act.dma_start(gate[:, :, :], gate_w.rearrange("(k p) e -> p k e", p=P)).then_inc(gate_in, 16)
            act.wait_ge(gains_in, 32)
            act.activation(gains[:, 2:4], gains[:, 0:2], ACT.Tanh).then_inc(tanh_done, 1)
            act.wait_ge(small_in, 32)
            act.activation(qb16[:, :], qb[:, :], ACT.Copy, scale=QSCALE).then_inc(qb_done, 1)
            act.wait_ge(wq_in, 16)
            act.activation(wqs[:, 0, :, :], wq[:, :, :], ACT.Copy, scale=QSCALE).then_inc(wq_hi, 1)
            for g in range(NG):
                act.wait_ge(k_ps, 1)
                act.activation(kTf[:, g, :], pQ[:, g * B * LK:(g + 1) * B * LK], ACT.Identity,
                               bias=kb[:, g:g + 1]).then_inc(k_sb, 1)
            act.wait_ge(k_sb, NG)
            act.activation(kTs[:, 0, :, :], kTf[:, :, :], ACT.Copy).then_inc(kT_hi, 1)
            act.wait_ge(qb_done, 1)

            def weight_high(s, u):
                e = expert_of(act, s)
                for c in range(2):
                    act.wait_ge(w_in[c], (s + 1) * 16)
                    if u % 2 == 0:
                        hi = W1[:, at(e), 0, c, :].rearrange("p o f -> p (o f)")
                    else:
                        hi = W2[:, at(e), 0, c * KF // 2:(c + 1) * KF // 2, :].rearrange("p o f d -> p (o f d)")
                    act.activation(hi, stage[:, c, :], ACT.Copy, scale=WSCALE).then_inc(w_hi, 1)

            def step(s, u, grp):
                t, a = s, u % 2
                if live(t):
                    act.wait_ge(xnT_ps, t + 1)
                    if some(t - 1):
                        act.wait_ge(q_ps, t - 1)
                    act.activation(xnT[:, a, 0, :, :], pT[:, 0:KD * P].rearrange("p (k n) -> p k n", k=KD),
                                   ACT.Copy).then_inc(xnT_hi, 1)
                t, a = s - 2, u % 2
                if live(t):
                    for r in range(3):
                        act.wait_ge(pt_ps, t * 3 + r + 1)
                        if r == 0:
                            if some(t):
                                act.wait_ge(o_ps, t)
                        lo_c, hi_c = 4 * r, min(4 * r + 4, NC)
                        full = hi_c if hi_c < NC else NC - 1
                        last = act.activation(probT[:, lo_c * P:full * P], pP[:, r % 2, 0:(full - lo_c) * P], ACT.Copy)
                        if hi_c == NC:
                            last = act.activation(probT[0:TAIL, full * P:NC * P],
                                                  pP[0:TAIL, r % 2, (full - lo_c) * P:(NC - lo_c) * P], ACT.Copy)
                        last.then_inc(pt_sb, 1)
                t, a = s - 1, (u + 1) % 2
                if live(t):
                    act.wait_ge(shift_done, t * 2 + 2)
                    act.activation(prob[:, a, :], prob[:, a, :], ACT.Exp,
                                   scale=float(HD) ** -0.5 / QSCALE).then_inc(prob_ready, 1)
                t, a = s, u % 2
                if live(t):
                    act.wait_ge(q_ps, t + 1)
                    if some(t - 1):
                        act.wait_ge(s_ps, t - 1)
                    for g in range(NG):
                        act.activation(qT[:, a, 0, g, :], pQ[:, g * P:(g + 1) * P], ACT.Identity,
                                       bias=qb16[:, g:g + 1]).then_inc(q_hi, 1)
                t, a = s - 3, (u + 1) % 2
                if live(t):
                    act.wait_ge(xn2T_ps, t + 1)
                    if some(t):
                        act.wait_ge(logit_ps, t)
                    act.activation(xn2T[:, a, :], pT[:, 0:D], ACT.Copy).then_inc(xn2T_sb, 1)
                if live(s):
                    weight_high(s, u)
                if grp is not None:
                    act.wait_ge(route_done, grp * 26 + 2)
                    act.activation(rt["exp"][:, :, :], rt["shift"][:, :, :], ACT.Exp).then_inc(exp_ready, 1)

            attention_steps(act, step)

            def gelu(j):
                for q in range(NQ):
                    act.wait_ge(h_ps, j * NQ + q + 1)
                    if some(j * NQ + q + 1 - NQ):
                        act.wait_ge(h_lo, j * NQ + q + 1 - NQ)
                    act.activation(hid[:, q, :], hbank[q][:, 0:512], ACT.Gelu_apprx_tanh,
                                   scale=1.0 / WSCALE).then_inc(h_act, 1)

            def y_copy(j, a, i):
                act.wait_ge(h_used, (j + 1) * NQ)
                if some(i * 16):
                    act.wait_ge(y_out[a], i * 16)
                act.activation(yb[:, a, :, :].rearrange("p h d -> p (h d)"), ybank[a], ACT.Copy).then_inc(y_sb, 1)

            gelu(0)
            gelu(1)
            y_copy(0, 0, 0)
            gelu(2)
            y_copy(1, 1, 0)
            with act.Fori(0, (NB - 3) // MU) as i:
                for u in range(MU):
                    gelu(i * MU + u + 3)
                    y_copy(i * MU + u + 2, u % 2, i * (MU // 2) + u // 2 + 1)
            y_copy(NB - 1, (NB - 1) % 2, (NB - 1) // 2)

        @block.tensor
        def _(pe):
            pe.wait_ge(kv_in, 64)
            for g in range(NG):
                for k in range(KD):
                    mm = pe.matmul(pQ[:, g * B * LK:(g + 1) * B * LK], wk[:, k, g * P:(g + 1) * P], cT[:, k, :],
                                   start=(k == 0), stop=(k == KD - 1))
            mm.then_inc(k_ps, 1)
            for b in range(B):
                for k in range(KD):
                    mm = pe.matmul(pS[0:LK, b, 0:D], cT[:, k, b * LK:(b + 1) * LK], wv[:, k, :],
                                   start=(k == 0), stop=(k == KD - 1))
            mm.then_inc(v_ps, 1)
            pe.wait_ge(vaug_done, B)
            pe.wait_ge(chunk_made, -(-(LK + P) // LK))
            pe.wait_ge(const_made, CONSTS)
            for b in range(B):
                for c in range(NC):
                    r0 = P * c % LK
                    mm = pe.matmul(pP[:, b, c * CH * VW:(c + 1) * CH * VW], spread[0:LK, r0:r0 + P],
                                   vaug[0:LK, b, head0[c]:head0[c] + CH, :].rearrange("p h w -> p (h w)"),
                                   start=True, stop=True)
            mm.then_inc(vc_ps, 1)
            pe.wait_ge(ident_made, 2)
            pe.wait_ge(wq_lo, 1)
            pe.wait_ge(kbd_done, B * NG * 2)
            pe.wait_ge(mask_done, 1)
            pe.wait_ge(k_sb, NG)
            pe.wait_ge(vbd_done, B)
            pe.wait_ge(gate_in, 16)

            def step(s, u, grp):
                t, a = s, u % 2
                if live(t):
                    pe.wait_ge(xn_ready, t + 1)
                    if some(t):
                        pe.wait_ge(xnT_lo, t)
                    if some(t - 3):
                        pe.wait_ge(xn2T_sb, t - 3)
                    for k in range(KD):
                        mm = pe.transpose(pT[:, k * P:(k + 1) * P], xn[:, a, k * P:(k + 1) * P], ident[:, :])
                    mm.then_inc(xnT_ps, 1)
                t, a = s - 1, (u + 1) % 2
                if live(t):
                    b = batch_of(pe, t)
                    pe.wait_ge(q_lo, NG * (t + 1))
                    if some(t * 2):
                        pe.wait_ge(shift_done, t * 2)
                    for bank, col, g, h0, nh in PARTS:
                        dst = pS[:, bank, col:col + nh * LK]
                        pe.matmul(dst, ones[0:1, :], maskrow[:, at(b), :, :].rearrange("p b o k -> p (b o) k").broadcast_to([1, nh, LK]),
                                  start=True, stop=False)
                        for qs, ks in ((0, 0), (0, 1), (1, 0)):
                            mm = pe.matmul(dst, qT[:, a, qs, g, :],
                                           kbd[:, at(b), g, ks, h0 * LK:(h0 + nh) * LK].rearrange("p o n -> p (o n)"),
                                           start=False, stop=(qs == 1))
                    mm.then_inc(s_ps, 1)
                t, a = s - 2, u % 2
                if live(t):
                    b = batch_of(pe, t)
                    pe.wait_ge(prob_ready, t + 1)
                    for r in range(3):
                        if some(t * 3 + max(r - 1, 0)):
                            pe.wait_ge(pt_sb, t * 3 + max(r - 1, 0))
                        for c in range(4 * r, min(4 * r + 4, NC)):
                            n = P if c < NC - 1 else TAIL
                            mm = pe.transpose(pP[0:n, r % 2, (c - 4 * r) * P:(c - 4 * r + 1) * P],
                                              prob[:, a, c * P:c * P + n], ident[:, :])
                        mm.then_inc(pt_ps, 1)
                    if some(t):
                        pe.wait_ge(att_done, t)
                    for c in range(NC):
                        if c % 4 == 0:
                            pe.wait_ge(pt_sb, t * 3 + c // 4 + 1)
                        n = P if c < NC - 1 else TAIL
                        mm = pe.matmul(pO[:, head0[c] * VW:(head0[c] + CH) * VW], probT[0:n, c * P:(c + 1) * P],
                                       vbd[0:n, at(b), c, :].rearrange("p o n -> p (o n)"),
                                       start=(c == 0), stop=(c == NC - 1), skip_group_check=True)
                    mm.then_inc(o_ps, 1)
                t, a = s, u % 2
                if live(t):
                    pe.wait_ge(xnT_lo, t + 1)
                    if some(t - 3):
                        pe.wait_ge(logit_sb, t - 3)
                    if some(NG * t):
                        pe.wait_ge(q_lo, NG * t)
                    for g in range(NG):
                        for n, (ws, k, xp) in enumerate([(ws, k, xp) for k in range(KD)
                                                         for ws, xp in ((0, 0), (0, 1), (1, 0))]):
                            mm = pe.matmul(pQ[:, g * P:(g + 1) * P], wqs[:, ws, k, g * P:(g + 1) * P],
                                           xnT[:, a, xp, k, :], start=(n == 0), stop=(n == 3 * KD - 1))
                    mm.then_inc(q_ps, 1)
                t, a = s - 3, (u + 1) % 2
                if live(t):
                    r = (u - DEPTH) % GT
                    pe.wait_ge(xn2_ready, t + 1)
                    if isinstance(s, int):
                        pe.wait_ge(xnT_lo, min(s + 1, NT))
                    else:
                        pe.wait_ge(xnT_lo, s + 1)
                    if some(t):
                        pe.wait_ge(xn2T_sb, t)
                    for k in range(KD):
                        mm = pe.transpose(pT[:, k * P:(k + 1) * P], xn2[:, r, k * P:(k + 1) * P], ident[:, :])
                    mm.then_inc(xn2T_ps, 1)
                    pe.wait_ge(xn2T_sb, t + 1)
                    pe.wait_ge(q_lo, NG * min(s + 1, NT) if isinstance(s, int) else (s + 1) * NG)
                    if some(t):
                        pe.wait_ge(logit_sb, t)
                    for k in range(KD):
                        mm = pe.matmul(pQ[:, 0:E], xn2T[:, a, k * P:(k + 1) * P], gate[:, k, :],
                                       start=(k == 0), stop=(k == KD - 1))
                    mm.then_inc(logit_ps, 1)
                if grp is not None:
                    pe.wait_ge(pick_ready, grp + 1)
                    if some(min(s - 2, NT) if isinstance(s, int) else s - 2):
                        pe.wait_ge(logit_sb, min(s - 2, NT) if isinstance(s, int) else s - 2)
                    for k in range(GT + 1):
                        for m in range(min(k, GT)):
                            mm = pe.matmul(pQ[:, k * E:(k + 1) * E], ones[:, :], pick16[:, m, :],
                                           start=(m == 0), stop=(k == GT and m == GT - 1))
                        if k < GT:
                            mm = pe.matmul(pQ[:, k * E:(k + 1) * E], before[:, :], pick16[:, k, :],
                                           start=(k == 0), stop=True)
                    mm.then_inc(rank_ps, 1)
                    pe.wait_ge(rank_used, grp + 1)

            attention_steps(pe, step)

            pe.wait_ge(blk_ready, 3)
            pe.wait_ge(w_lo, WCH)
            ereg = pe.alloc_register("block_expert")

            def load_x(j, a, i):
                pe.wait_ge(xb_in[a], (i + 1) * 16)
                if some(j - 1):
                    pe.wait_ge(xbT_sb, j - 1)
                for h in range(MH):
                    for n in range(2 * KD):
                        mm = pe.transpose(tbank[a].bitcast(F16)[:, n * MB + h * P:n * MB + (h + 1) * P],
                                          xb[:, a, h, n * P:(n + 1) * P], ident16[:, :])
                mm.then_inc(xbT_ps, 1)

            def up(j, a):
                pe.reg_load(ereg, blk[0:1, 0, at(j)])
                e = pe.snap(ereg, min_val=0, max_val=E - 1)
                pe.wait_ge(xbT_sb, j + 1)
                for q in range(NQ):
                    if some(j * NQ + q + 1 - NQ):
                        pe.wait_ge(h_act, j * NQ + q + 1 - NQ)
                    for f in range(QF * q, QF * (q + 1)):
                        dst = hbank[q][:, (f % QF) * MB:(f % QF + 1) * MB]
                        for n, (k, ws, xp) in enumerate([(k, ws, xp) for k in range(KD)
                                                         for ws, xp in ((0, 0), (0, 1), (1, 0))]):
                            mm = pe.matmul(dst, W1[:, at(e), ws, k, f * P:(f + 1) * P].rearrange("p o n -> p (o n)"),
                                           xbT[:, a, xp, k, :], start=(n == 0), stop=(n == 3 * KD - 1))
                    mm.then_inc(h_ps, 1)

            def down(j, a):
                pe.reg_load(ereg, blk[0:1, 0, at(j)])
                e = pe.snap(ereg, min_val=0, max_val=E - 1)
                if some(j - 1):
                    pe.wait_ge(y_sb, j - 1)
                for q in range(NQ):
                    pe.wait_ge(h_lo, j * NQ + q + 1)
                    for f in range(QF * q, QF * (q + 1)):
                        for hp, ws in ((0, 0), (1, 0), (0, 1)):
                            for h in range(MH):
                                mm = pe.matmul(ybank[a][:, h * D:(h + 1) * D],
                                               hidS[:, q, hp, (f % QF) * MB + h * P:(f % QF) * MB + (h + 1) * P],
                                               W2[:, at(e), ws, f, :].rearrange("p o n -> p (o n)"),
                                               start=(f + hp + ws + h == 0),
                                               stop=(f == KF - 1 and ws == 1 and h == MH - 1), skip_group_check=True)
                    mm.then_inc(h_used, 1)

            load_x(0, 0, 0)
            load_x(1, 1, 0)
            up(0, 0)
            load_x(2, 0, 1)
            up(1, 1)
            down(0, 0)
            with pe.Fori(0, (NB - 3) // MU) as i:
                for u in range(MU):
                    j = i * MU + u + 2
                    load_x(j + 1, (u + 1) % 2, i * (MU // 2) + (u + 3) // 2)
                    up(j, u % 2)
                    down(j - 1, (u + 1) % 2)
            up(NB - 1, (NB - 1) % 2)
            down(NB - 2, NB % 2)
            down(NB - 1, (NB - 1) % 2)

        @block.vector
        def _(dve):
            for c in range(4):
                dve.wait_ge(x_in, 16 * (c + 1))
                for t in range(c * NT // 4, (c + 1) * NT // 4):
                    dve.bn_stats(stat1[:, t, :], X[:, t, :]).then_inc(stat1_done, 1)
            for t in range(NT):
                dve.wait_ge(stat1_done, t + 1)
                dve.bn_aggr(mv1[:, t, :], stat1[:, t, :]).then_inc(mv1_done, 1)
            dve.wait_ge(wq_hi, 1)
            dve.scalar_tensor_tensor(out=wqs[:, 1, :, :], in0=wq[:, :, :], scalar=QSCALE, in1=wqs[:, 0, :, :],
                                     op0=ALU.mult, op1=ALU.subtract).then_inc(wq_lo, 1)
            dve.wait_ge(kT_hi, 1)
            dve.tensor_tensor(kTs[:, 1, :, :], kTf[:, :, :], kTs[:, 0, :, :], ALU.subtract).then_inc(kT_lo, 1)
            dve.wait_ge(v_ps, 1)
            dve.wait_ge(const_made, CONSTS)
            for b in range(B):
                dve.tensor_tensor(vaug[0:LK, b, :, 0:HD], pS[0:LK, b, 0:D].rearrange("p (h w) -> p h w", h=H),
                                  vb[0:LK, :].rearrange("p (h w) -> p h w", h=H), ALU.add).then_inc(vaug_done, 1)
            dve.wait_ge(mask_in, 16)
            dve.tensor_scalar(maskrow[:, :, 0, :], maski[:, :, :],
                              0.0, MASKED, ALU.is_gt, ALU.mult).then_inc(mask_done, 1)
            dve.wait_ge(vc_ps, 1)
            dve.wait_ge(chunk_made, -(-(LK + P) // LK) + 2 * NC + 7)
            for b in range(B):
                dve.tensor_tensor(vbd[:, b, :, :].rearrange("p c (h w) -> p c h w", h=CH),
                                  pP[:, b, 0:NC * CH * VW].rearrange("p (c h w) -> p c h w", c=NC, h=CH),
                                  chunkm[:, :, :].rearrange("p c (h o) -> p c h o", o=1).broadcast_to([P, NC, CH, VW]),
                                  ALU.mult).then_inc(vbd_done, 1)
            dve.wait_ge(tanh_done, 1)
            dve.tensor_scalar(gffn[:, :], gains[:, 3:4], 1.0 / WSCALE, None, ALU.mult).then_inc(final_done, 1)
            dve.wait_ge(final_done, 1)
            dve.wait_ge(qb_done, 1)

            def route_group(g, t0):
                R, V = rt, rv
                base = g * 26
                n = 0

                def done(ins):
                    nonlocal n
                    n += 1
                    ins.then_inc(route_done, 1)

                def after():
                    dve.wait_ge(route_done, base + n)

                def wide(v):
                    return v.rearrange("p (t o) -> p t o", o=1).broadcast_to([P, GT, E])

                dsc = desc[:, :].rearrange("p (o e) -> p o e", o=1).broadcast_to([P, GT, E])
                oh1 = chosen[:, 0, at(t0, GT), :]
                oh2 = chosen[:, 1, at(t0, GT), :]
                lg = logit[:, at(t0, GT), :]
                done(dve.tensor_reduce(V["max"][:, :], lg, AX.X, ALU.max))
                after()
                done(dve.tensor_tensor(R["shift"][:, :, :], lg, wide(V["max"][:, :]), ALU.subtract))
                dve.wait_ge(exp_ready, g + 1)
                done(dve.tensor_reduce(V["sum"][:, :], R["exp"][:, :, :], AX.X, ALU.add))
                after()
                done(dve.reciprocal(V["rsum"][:, :], V["sum"][:, :]))
                after()
                done(dve.tensor_tensor(R["p"][:, :, :], R["exp"][:, :, :], wide(V["rsum"][:, :]), ALU.mult))
                after()
                done(dve.tensor_reduce(V["m1"][:, :], R["p"][:, :, :], AX.X, ALU.max))
                after()
                done(dve.tensor_tensor(R["eq"][:, :, :], R["p"][:, :, :], wide(V["m1"][:, :]), ALU.is_equal))
                after()
                done(dve.tensor_tensor(R["c"][:, :, :], R["eq"][:, :, :], dsc, ALU.mult))
                after()
                done(dve.tensor_reduce(V["f1"][:, :], R["c"][:, :, :], AX.X, ALU.max))
                after()
                done(dve.tensor_tensor(oh1, dsc, wide(V["f1"][:, :]), ALU.is_equal))
                after()
                done(dve.scalar_tensor_tensor(out=R["p2"][:, :, :], in0=oh1, scalar=-2.0, in1=R["p"][:, :, :],
                                              op0=ALU.mult, op1=ALU.add))
                after()
                done(dve.tensor_reduce(V["m2"][:, :], R["p2"][:, :, :], AX.X, ALU.max))
                after()
                done(dve.tensor_tensor(R["eq"][:, :, :], R["p2"][:, :, :], wide(V["m2"][:, :]), ALU.is_equal))
                after()
                done(dve.tensor_tensor(R["c"][:, :, :], R["eq"][:, :, :], dsc, ALU.mult))
                after()
                done(dve.tensor_reduce(V["f2"][:, :], R["c"][:, :, :], AX.X, ALU.max))
                after()
                done(dve.tensor_tensor(oh2, dsc, wide(V["f2"][:, :]), ALU.is_equal))
                after()
                dve.tensor_tensor(pick16[:, :, :], oh1, oh2, ALU.add).then_inc(pick_ready, 1)
                done(dve.tensor_tensor(V["ws"][:, :], V["m1"][:, :], V["m2"][:, :], ALU.add))
                after()
                done(dve.reciprocal(V["rws"][:, :], V["ws"][:, :]))
                after()
                for c, m in enumerate(("m1", "m2")):
                    done(dve.scalar_tensor_tensor(out=comb[:, c, at(t0, GT)], in0=V[m][:, :], scalar=gffn[:, 0:1],
                                                  in1=V["rws"][:, :], op0=ALU.mult, op1=ALU.mult))
                dve.wait_ge(rank_ps, g + 1)
                done(dve.tensor_tensor(R["rank"][:, :, :], pQ[:, 0:GT * E].rearrange("p (t e) -> p t e", t=GT),
                                       count[:, :].rearrange("p (o e) -> p o e", o=1).broadcast_to([P, GT, E]), ALU.add))
                after()
                dve.tensor_tensor(count[:, :], pQ[:, GT * E:(GT + 1) * E], count[:, :], ALU.add).then_inc(rank_used, 1)
                dve.wait_ge(rank_used, g + 1)
                done(dve.tensor_tensor(R["rank"][:, :, :], R["rank"][:, :, :],
                                       eoff[:, :].rearrange("p (o e) -> p o e", o=1).broadcast_to([P, GT, E]), ALU.add))
                after()
                done(dve.tensor_tensor(R["s1"][:, :, :], R["rank"][:, :, :], oh1, ALU.mult))
                done(dve.tensor_tensor(R["s2"][:, :, :], R["rank"][:, :, :], oh2, ALU.mult))
                after()
                done(dve.tensor_reduce(slot[:, 0, at(t0, GT)], R["s1"][:, :, :], AX.X, ALU.add))
                done(dve.tensor_reduce(slot[:, 1, at(t0, GT)], R["s2"][:, :, :], AX.X, ALU.add))
                after()
                dve.wait_ge(row_hi, t0 + 1)
                dve.tensor_scalar(sloti[:, :, :], slot[:, :, at(t0, GT)], 0.0, None, ALU.add).then_inc(slots_ready, 1)
                assert n == 26, n

            def normalise(t, a):
                if some(t - 1):
                    dve.wait_ge(xnT_ps, t - 1)
                dve.tensor_scalar(xn[:, a, :], X[:, at(t), :].rearrange("p o d -> p (o d)"),
                                  mv1[:, at(t), 0], rstd1[:, at(t)], ALU.subtract,
                                  ALU.mult).then_inc(xn_ready, 1)

            dve.wait_ge(rstd1_done, 1)

            def step(s, u, grp):
                if live(s):
                    normalise(s, u % 2)
                t, a = s - 1, (u + 1) % 2
                if live(t):
                    dve.wait_ge(s_ps, t + 1)
                    nb2 = 2 * HB
                    dve.tensor_reduce(mx[:, a, 0:nb2].rearrange("p (b h) -> p b h", b=2),
                                      pS[:, 0:2, 0:HB * LK].rearrange("p b (h k) -> p b h k", h=HB),
                                      AX.X, ALU.max).then_inc(max_done, 1)
                    dve.tensor_reduce(mx[:, a, nb2:H], pS[:, 2, 0:(H - nb2) * LK].rearrange("p (h k) -> p h k", k=LK),
                                      AX.X, ALU.max).then_inc(max_done, 1)
                    dve.wait_ge(max_done, t * 2 + 2)
                    if some(t * 3 - 3):
                        dve.wait_ge(pt_ps, t * 3 - 3)
                    dve.tensor_tensor(prob[:, a, 0:nb2 * LK].rearrange("p (b h k) -> p b h k", b=2, h=HB),
                                      pS[:, 0:2, 0:HB * LK].rearrange("p b (h k) -> p b h k", h=HB),
                                      mx[:, a, 0:nb2].rearrange("p (b h o) -> p b h o", b=2, o=1).broadcast_to([P, 2, HB, LK]),
                                      ALU.subtract).then_inc(shift_done, 1)
                    dve.tensor_tensor(prob[:, a, nb2 * LK:HK].rearrange("p (h k) -> p h k", k=LK),
                                      pS[:, 2, 0:(H - nb2) * LK].rearrange("p (h k) -> p h k", k=LK),
                                      mx[:, a, nb2:H].rearrange("p (h o) -> p h o", o=1).broadcast_to([P, H - nb2, LK]),
                                      ALU.subtract).then_inc(shift_done, 1)
                t, a = s, u % 2
                if live(t):
                    dve.wait_ge(xnT_hi, t + 1)
                    dve.tensor_tensor(xnT[:, a, 1, :, :], pT[:, 0:KD * P].rearrange("p (k n) -> p k n", k=KD),
                                      xnT[:, a, 0, :, :], ALU.subtract).then_inc(xnT_lo, 1)
                t, a, r = s - 2, u % 2, (u - 2) % GT
                if live(t):
                    dve.wait_ge(o_ps, t + 1)
                    heads = pO[:, 0:H * VW].rearrange("p (h w) -> p h w", h=H)
                    dve.reciprocal(rsum[:, a, :], heads[:, :, HD]).then_inc(rsum_done, 1)
                    dve.wait_ge(rsum_done, t + 1)
                    dve.tensor_tensor(att[:, :].rearrange("p (h w) -> p h w", h=H), heads[:, :, 0:HD],
                                      rsum[:, a, :].rearrange("p (h o) -> p h o", o=1).broadcast_to([P, H, HD]),
                                      ALU.mult).then_inc(att_done, 1)
                    dve.wait_ge(att_done, t + 1)
                    dve.wait_ge(xn_ready, t + 1)
                    xt = X[:, at(t), :].rearrange("p o d -> p (o d)")
                    dve.scalar_tensor_tensor(out=xt, in0=att[:, :], scalar=gains[:, 2:3], in1=xt,
                                             op0=ALU.mult, op1=ALU.add).then_inc(x1_done, 1)
                    n = dve.snap(t + 1)
                    dve.wait_ge(const_made, CONSTS)
                    dve.wait_ge(x1_done, n)
                    dve.bn_stats(stat2[:, a, :], xt).then_inc(stat2_done, 1)
                    n = dve.snap(t + 1)
                    dve.wait_ge(const_made, CONSTS)
                    dve.wait_ge(stat2_done, n)
                    dve.bn_aggr(mv2[:, a, :], stat2[:, a, :]).then_inc(mv2_done, 1)
                    dve.wait_ge(mv2_done, t + 1)
                    dve.tensor_scalar(ve2[:, a, :], mv2[:, a, 1:2], EPS, None, ALU.add).then_inc(ve2_done, 1)
                    dve.wait_ge(rstd2_done, t + 1)
                    if some(t - 1):
                        dve.wait_ge(xn2T_ps, t - 1)
                    if isinstance(s, int):
                        if some(t - GT + 1):
                            dve.wait_ge(row_lo, t - GT + 1)
                    else:
                        if some((s - 1) * 2):
                            dve.wait_ge(w_lo, (s - 1) * 2)
                    dve.tensor_scalar(xn2[:, r, :], xt, mv2[:, a, 0:1], rstd2[:, a, :], ALU.subtract,
                                      ALU.mult).then_inc(xn2_ready, 1)
                t, a = s, u % 2
                if live(t):
                    dve.wait_ge(q_hi, NG * (t + 1))
                    for g in range(NG):
                        dve.scalar_tensor_tensor(out=qT[:, a, 1, g, :], in0=pQ[:, g * P:(g + 1) * P],
                                                 scalar=qb16[:, g:g + 1], in1=qT[:, a, 0, g, :],
                                                 op0=ALU.add, op1=ALU.subtract).then_inc(q_lo, 1)
                t = s - 3
                if live(t):
                    n = dve.snap(t + 1)
                    dve.wait_ge(const_made, CONSTS)
                    dve.wait_ge(logit_ps, n)
                    dve.tensor_copy(logit[:, at(t), :].rearrange("p o e -> p (o e)"), pQ[:, 0:E]).then_inc(logit_sb, 1)
                    dve.wait_ge(logit_sb, t + 1)
                if grp is not None:
                    route_group(grp, s - (2 * UNROLL - 1))

            attention_steps(dve, step)

            nfin = 1

            def fin(ins):
                nonlocal nfin
                nfin += 1
                ins.then_inc(final_done, 1)
                dve.wait_ge(final_done, nfin)

            def blkdone(ins):
                ins.then_inc(blk_ready, 1)

            dve.wait_ge(w_lo, WCH)
            dve.wait_ge(zero_made, 3)
            fin(dve.tensor_tensor(over[:, :, :], count[:, :].rearrange("p (e o) -> p e o", o=1).broadcast_to([P, E, NT]),
                                  kstep[:, :].rearrange("p (o k) -> p o k", o=1).broadcast_to([P, E, NT]), ALU.is_gt))
            dve.tensor_tensor(padrow[:, :], count[0:1, :], eoff[0:1, :], ALU.add).then_inc(max_done, 1)
            dve.wait_ge(max_done, 2 * NT + 1)
            blkdone(dve.tensor_copy(padi[:, :], padrow[:, :]))
            fin(dve.tensor_reduce(nblk[:, :], over[:, :, :], AX.X, ALU.add))
            fin(dve.tensor_tensor(cum[:, :, :], nblk[:, :].rearrange("p (o e) -> p o e", o=1).broadcast_to([P, E, E]),
                                  upto[:, :, :], ALU.mult))
            fin(dve.tensor_reduce(end[:, :], cum[:, :, :], AX.X, ALU.add))
            j_wide = jstep[:, :].rearrange("p (j o) -> p j o", o=1).broadcast_to([1, NB, E])
            chain = 2 * NT + 1

            def link(ins):
                nonlocal chain
                chain += 1
                ins.then_inc(max_done, 1)
                dve.wait_ge(max_done, chain)

            link(dve.tensor_tensor(past[:, :, :], j_wide,
                                   end[0:1, :].rearrange("p (o e) -> p o e", o=1).broadcast_to([1, NB, E]), ALU.is_ge))
            link(dve.memset(coef[:, E - 1:E], float(DUMP)))
            link(dve.tensor_scalar(coef[:, 0:E - 1], nblk[0:1, 0:E - 1], -float(MB), float(CAP), ALU.mult, ALU.add))
            link(dve.tensor_reduce(bexp, past[:, :, 0:E - 1], AX.X, ALU.add))
            link(dve.tensor_tensor(pastc[:, :, :], past[:, :, :],
                                   coef[:, :].rearrange("p (o e) -> p o e", o=1).broadcast_to([1, NB, E]), ALU.mult))
            blkdone(dve.tensor_copy(blk[:, 0, :], bexp))
            link(dve.tensor_reduce(brow[:, 0, :], pastc[:, :, :], AX.X, ALU.add))
            link(dve.scalar_tensor_tensor(out=brow[:, 1, :], in0=jstep[:, :], scalar=float(MB), in1=brow[:, 0, :],
                                          op0=ALU.mult, op1=ALU.add))
            blkdone(dve.tensor_scalar(blk[:, 1, :], brow[:, 1, :], float(DUMP), None, ALU.min))
            link(dve.tensor_tensor(delta[:, 0, :], end[:, :], nblk[:, :], ALU.subtract))
            link(dve.scalar_tensor_tensor(out=delta[:, 1, :], in0=delta[:, 0, :], scalar=float(MB), in1=eoff[:, :],
                                          op0=ALU.mult, op1=ALU.subtract))
            for c in range(2):
                link(dve.tensor_tensor(cd[:, c, :, :], chosen[:, c, :, :],
                                       delta[:, 1, :].rearrange("p (o e) -> p o e", o=1).broadcast_to([P, NT, E]), ALU.mult))
            link(dve.tensor_reduce(cdr[:, :, :], cd[:, :, :, :], AX.X, ALU.add))
            fin(dve.tensor_tensor(cslot[:, :, :], cdr[:, :, :], slot[:, :, :], ALU.add))
            fin(dve.tensor_copy(csloti[:, :, :], cslot[:, :, :]))
            assert nfin == 7, nfin

            def xb_copy(j, a):
                dve.wait_ge(xbT_ps, j + 1)
                if some(j * NQ - NQ):
                    dve.wait_ge(h_ps, j * NQ - NQ)
                dve.tensor_copy(xbT[:, a, :, :, :].rearrange("p s k n -> p (s k n)"),
                                tbank[a].bitcast(F16)).then_inc(xbT_sb, 1)

            def split(j):
                for q in range(NQ):
                    dve.wait_ge(h_act, j * NQ + q + 1)
                    if some(j * NQ + q + 1 - NQ):
                        dve.wait_ge(h_used, j * NQ + q + 1 - NQ)
                    dve.tensor_copy(hidS[:, q, 0, :], hid[:, q, :]).then_inc(h_hi, 1)
                    dve.wait_ge(h_hi, j * NQ + q + 1)
                    dve.tensor_tensor(hidS[:, q, 1, :], hid[:, q, :], hidS[:, q, 0, :], ALU.subtract).then_inc(h_lo, 1)

            xb_copy(0, 0)
            xb_copy(1, 1)
            split(0)
            xb_copy(2, 0)
            split(1)
            with dve.Fori(0, (NB - 3) // MU) as i:
                for u in range(MU):
                    xb_copy(i * MU + u + 3, (u + 1) % 2)
                    split(i * MU + u + 2)
            split(NB - 1)

            def combine(t, a, r, i):
                dve.wait_ge(pick_in[a], (i + 1) * 32)
                if some((i * 2 + a // 2) * 16):
                    dve.wait_ge(out_sent[r], (i * 2 + a // 2) * 16)
                xt = X[:, at(t), :].rearrange("p o d -> p (o d)")
                dve.scalar_tensor_tensor(out=part[:, r, :], in0=picks[:, a, 0, :], scalar=comb[:, 0, at(t)], in1=xt,
                                         op0=ALU.mult, op1=ALU.add).then_inc(part_done, 1)
                dve.wait_ge(part_done, t + 1)
                dve.scalar_tensor_tensor(out=res[:, r, :], in0=picks[:, a, 1, :], scalar=comb[:, 1, at(t)],
                                         in1=part[:, r, :], op0=ALU.mult, op1=ALU.add).then_inc(res_done, 1)

            for t in range(4):
                combine(t, t, t % 2, 0)
            with dve.Fori(1, NT // 4) as i:
                for a in range(4):
                    combine(i * 4 + a, a, a % 2, i)


def kernel(**inputs):
    import numpy as np
    import concourse.bacc as bacc
    from concourse.bass_utils import run_bass_kernel_spmd as run

    def laid(a):
        return np.ascontiguousarray(a)

    nc = bacc.Bacc("TRN2", target_bir_lowering=False, num_devices=1)
    ctx = np.asarray(inputs["ctx_1024"])
    given = {
        "x": laid(inputs["x"]),
        "ctxT": laid(ctx.reshape(-1, ctx.shape[-1]).T),
        "mask": laid(inputs["mask_BxS2_ik0"]),
        "g_xattn": laid(inputs["g_xattn"]),
        "g_ffn": laid(inputs["g_ffn"]),
        "wqT": laid(np.asarray(inputs["L0_xattn_q_w"]).T),
        "q_b": laid(np.asarray(inputs["L0_xattn_q_b"]).reshape(-1, P).T),
        "wkT": laid(np.asarray(inputs["L0_xattn_k_w"]).T),
        "k_b": laid(np.asarray(inputs["L0_xattn_k_b"]).reshape(-1, P).T),
        "wvT": laid(np.asarray(inputs["L0_xattn_v_w"]).T),
        "v_b": laid(inputs["L0_xattn_v_b"]),
        "gate_w": laid(inputs["L0_ffn_gate_w"]),
        "w1": laid(inputs["L0_ffn_w1"]),
        "w2": laid(inputs["L0_ffn_w2"]),
    }
    args = [nc.dram_tensor("in_" + n, a.shape, mybir.dt.from_np(a.dtype), kind="ExternalInput").ap()
            for n, a in given.items()]
    out = nc.dram_tensor("out_0", given["x"].shape, F32, kind="ExternalOutput").ap()
    flamingo_moe_block(nc, *args, out)
    r = run(nc, [{"in_" + n: a for n, a in given.items()}], core_ids=[0])
    return r.results[0]["out_0"]
```

```python
from contextlib import ExitStack

import concourse.bass as bass
from concourse import mybir

F32 = mybir.dt.float32
F16 = mybir.dt.float16
BF16 = mybir.dt.bfloat16
I32 = mybir.dt.int32
ACT = mybir.ActivationFunctionType
ALU = mybir.AluOpType
AX = mybir.AxisListType

P = 128
MB = 256
EPS = 1e-5
WSCALE = 256.0
QSCALE = 16.0
MASKED = -1.0e30
UNROLL = 4


def at(t, n=1):
    return bass.ds(t, n)


def flamingo_moe_block(nc, x, ctxT, mask, g_xattn, g_ffn, wqT, q_b, wkT, k_b, wvT, v_b, gate_w, w1, w2, out):
    B, L, D = x.shape
    LK = mask.shape[1]
    H, HD = 16, D // 16
    E, _, F = w1.shape
    NT = B * L // P
    TB = L // P
    KD = D // P
    KF = F // P
    HG = P // HD
    NG = H // HG
    GK = HG * LK
    HK = H * LK
    HB = 6
    NC = -(-HK // P)
    TAIL = HK - (NC - 1) * P
    VW = HD + 1
    CH = 3
    head0 = [min(P * c // LK, H - CH) for c in range(NC)]
    PARTS = [(0, 0, 0, 0, 6), (1, 0, 0, 6, 2), (1, 2 * LK, 1, 0, 4), (2, 0, 1, 4, 4)]
    NB = 2 * B * L // MB + E - 1
    MH = MB // P
    QF = 512 // MB
    NQ = KF // QF
    CAP = B * L + MB
    DUMP = (E - 1) * CAP + B * L
    GT = UNROLL
    CONSTS = 11
    POOL_LOW = (1,)
    WCH = 4 * E
    LG = PARTS[-1][1] + PARTS[-1][4] * LK

    xs = nc.dram_tensor("token_rows", [E * CAP, 2 * D], F16).ap()
    ys = nc.dram_tensor("expert_out", [NB * MB, D], F32).ap()

    with ExitStack() as ctx:
        def sb(name, shape, dt):
            return ctx.enter_context(nc.sbuf_tensor(name, shape, dt))

        def ps(name, shape, dt=F32):
            return ctx.enter_context(nc.psum_tensor(name, shape, dt))

        def sem(name):
            return ctx.enter_context(nc.semaphore(name))

        X = sb("X", [P, NT, D], F32)
        W = sb("W", [P, WCH + 2, 2, F], F16)
        Wf = W[:, :, :, :].rearrange("p n s f -> p (n s f)").bitcast(F32).rearrange("p (n f) -> p n f", f=F)
        We = W[:, 0:WCH, :, :].rearrange("p (e c) s f -> p e c s f", c=4)
        kbd = sb("kbd", [P, B, NG, 2, GK], F16)
        vbd = sb("vbd", [P, B, NC, CH * VW], F32)
        prob = sb("prob", [P, 2, HK], F32)
        probT = sb("probT", [P, NC * P], F32)
        rows = sb("rows", [P, GT, 2 * D], F16)
        xn = sb("xn", [P, 2, D], F32)
        xnT = sb("xnT", [P, 2, 2, KD, P], F16)
        qT = sb("qT", [P, 2, 2, NG, P], F16)
        att = sb("att", [P, D], F32)
        xn2 = sb("xn2", [P, GT, D], F32)
        xn2T = sb("xn2T", [P, 2, D], F32)
        wqs = sb("wqs", [P, 2, KD, D], F16)
        lent = {"probT": [probT[:, :], 0],
                "prob": [prob[:, :, :].rearrange("p a b -> p (a b)"), 0]}

        def setup_view(n, where="probT"):
            room, o = lent[where]
            lent[where][1] = o + n
            assert o + n <= room.shape[1]
            return room[:, o:o + n]

        wk = setup_view(KD * D, "prob").rearrange("p (k n) -> p k n", k=KD)
        wv = setup_view(KD * D, "prob").rearrange("p (k n) -> p k n", k=KD)
        cT = setup_view(KD * B * LK).rearrange("p (k n) -> p k n", k=KD)
        vaug = setup_view(B * H * VW).rearrange("p (b h w) -> p b h w", b=B, h=H)
        spread = setup_view(LK + P)
        maski = setup_view(B * LK)[0:1, :].bitcast(I32).rearrange("p (b k) -> p b k", b=B)
        vb = setup_view(D, "prob")
        wq = setup_view(KD * D, "prob").rearrange("p (k n) -> p k n", k=KD)
        kTf = setup_view(NG * B * LK, "prob").rearrange("p (g n) -> p g n", g=NG)
        kTs = setup_view(NG * B * LK, "prob").bitcast(F16).rearrange("p (s g n) -> p s g n", s=2, g=NG)
        spare = Wf[:, WCH:WCH + 2, :].rearrange("p n f -> p (n f)")
        lent["spare"] = [spare, 0]
        over = setup_view(E * NT, "spare").rearrange("p (e k) -> p e k", e=E)
        cum = setup_view(E * E, "spare").rearrange("p (e k) -> p e k", e=E)
        cd = setup_view(2 * NT * E, "spare").rearrange("p (c t e) -> p c t e", c=2, t=NT)
        past = setup_view(NB * E, "spare")[0:1, :].rearrange("p (j e) -> p j e", j=NB)
        pastc = setup_view(NB * E, "spare")[0:1, :].rearrange("p (j e) -> p j e", j=NB)
        zrows = setup_view(MH * D, "spare").bitcast(F16).rearrange("p (h d) -> p h d", h=MH)
        cdr = setup_view(2 * NT, "spare").rearrange("p (c t) -> p c t", c=2)
        cslot = setup_view(2 * NT, "spare").rearrange("p (c t) -> p c t", c=2)
        upto = setup_view(E * E, "spare").rearrange("p (e k) -> p e k", e=E)
        bexp = setup_view(NB, "spare")[0:1, :]
        brow = setup_view(2 * NB, "spare")[0:1, :].rearrange("p (s j) -> p s j", s=2)
        hid = lent["prob"][0][:, 0:NQ * 512].rearrange("p (q n) -> p q n", q=NQ)
        hidS = kbd[:, :, :, :, :].rearrange("p b g s n -> p (b g s n)")[:, 0:NQ * 2 * 512].rearrange(
            "p (q s n) -> p q s n", q=NQ, s=2)
        xb = rows[:, :, :].rearrange("p (a h) d -> p a h d", a=2)
        xbT = probT[:, 0:2 * D * MH].bitcast(F16).rearrange("p (a s k n) -> p a s k n", a=2, s=2, k=KD)
        rows_late = probT[:, 0:GT * D].bitcast(F16).rearrange("p (t d) -> p t d", t=GT)
        yb = xn2[:, :, :].rearrange("p (a h) d -> p a h d", a=2)
        picks = spare.rearrange("p (t c d) -> p t c d", c=2, d=D)
        gate = sb("gate", [P, KD, E], F32)
        ident = sb("ident", [P, P], F32)
        wscale = sb("wscale", [P, 1], F32)
        ident16 = sb("ident16", [P, P], F16)
        before = sb("before", [P, P], BF16)
        ones = sb("ones", [P, P], BF16)
        headm = sb("headm", [P, HG, 1], F32)
        chunkm = sb("chunkm", [P, NC, CH], F32)
        maskrow = sb("maskrow", [1, B, 1, LK], BF16)
        qb = sb("qb", [P, NG], F32)
        qb16 = sb("qb16", [P, NG], F32)
        kb = sb("kb", [P, NG], F32)
        gains = sb("gains", [P, 4], F32)
        gffn = sb("gffn", [P, 1], F32)
        iota_i = xn2[:, :, :].rearrange("p a d -> p (a d)")[:, 0:2 * NB].bitcast(I32).rearrange("p (s j) -> p s j", s=2)
        stat1 = xn2T[:, :, :].rearrange("p a d -> p (a d)")[:, 0:NT * 6].rearrange("p (t s) -> p t s", t=NT)
        mv1 = sb("mv1", [P, NT, 2], F32)
        ve1 = sb("ve1", [P, NT], F32)
        rstd1 = sb("rstd1", [P, NT], F32)
        neghalf = sb("neghalf", [P, NT], F32)
        held = sb("held", [P, 1], F32)
        mx = sb("mx", [P, 2, H], F32)
        rsum = sb("rsum", [P, 2, H], F32)
        stat2 = sb("stat2", [P, 2, 6], F32)
        mv2 = sb("mv2", [P, 2, 2], F32)
        ve2 = sb("ve2", [P, 2, 1], F32)
        rstd2 = sb("rstd2", [P, 2, 1], F32)
        logit = sb("logit", [P, NT, E], F32)
        rt = {n: sb("rt_" + n, [P, GT, E], F32) for n in
              ("shift", "exp", "p", "eq", "c", "p2", "rank", "s1", "s2")}
        rv = {n: sb("rv_" + n, [P, GT], F32) for n in
              ("max", "sum", "rsum", "m1", "f1", "m2", "f2", "ws", "rws")}
        chosen = sb("chosen", [P, 2, NT, E], BF16)
        pick16 = sb("pick16", [P, GT, E], BF16)
        comb = sb("comb", [P, 2, NT], F32)
        slot = sb("slot", [P, 2, NT], F32)
        sloti_late = sb("sloti_late", [P, 2, GT], I32)
        sloti = sb("sloti", [P, 2, GT], I32)
        count = sb("count", [P, E], F32)
        desc = sb("desc", [P, E], F32)
        eoff = sb("eoff", [P, E], F32)
        kstep = sb("kstep", [P, NT], F32)
        jstep = sb("jstep", [1, NB], F32)
        nblk = sb("nblk", [P, E], F32)
        end = sb("end", [P, E], F32)
        delta = sb("delta", [P, 2, E], F32)
        coef = sb("coef", [1, E], F32)
        blk = sb("blk", [1, 2, NB], I32)
        padrow = sb("padrow", [1, E], F32)
        padi = sb("padi", [1, E], I32)
        csloti = sb("csloti", [P, 2, NT], I32)
        part = xn
        res = qT[:, :, :, :, :].rearrange("p a s g n -> p a (s g n)").bitcast(F32)

        pT = ps("pT", [P, 512])
        pQ = ps("pQ", [P, 512])
        pS = ps("pS", [P, 3, 512])
        pP = ps("pP", [P, 2, 512])
        pO = ps("pO", [P, 512])
        hbank = [pQ, pS[:, 0, :], pS[:, 1, :], pS[:, 2, :]]
        ybank = [pP[:, 0, :], pP[:, 1, :]]
        tbank = [pT[:, :], pO[:, :]]

        x_in = [sem(f"x_in{i}") for i in range(4)]
        wq_in = sem("wq_in")
        kv_in = sem("kv_in")
        small_in = sem("small_in")
        gate_in = sem("gate_in")
        mask_in = sem("mask_in")
        gains_in = sem("gains_in")
        const_made = sem("const_made")
        ident_made = sem("ident_made")
        chunk_made = sem("chunk_made")
        head_made = sem("head_made")
        tanh_done = sem("tanh_done")
        qb_done = sem("qb_done")
        wq_hi = sem("wq_hi")
        wq_lo = sem("wq_lo")
        k_ps = sem("k_ps")
        k_sb = sem("k_sb")
        kT_hi = sem("kT_hi")
        kT_lo = sem("kT_lo")
        kbd_hi = sem("kbd_hi")
        kbd_done = sem("kbd_done")
        v_ps = sem("v_ps")
        vaug_done = sem("vaug_done")
        vc_ps = sem("vc_ps")
        vbd_done = sem("vbd_done")
        mask_done = sem("mask_done")
        stat1_done = sem("stat1_done")
        mv1_done = sem("mv1_done")
        ve1_done = sem("ve1_done")
        rstd1_done = sem("rstd1_done")
        xn_ready = sem("xn_ready")
        xnT_ps = sem("xnT_ps")
        xnT_hi = sem("xnT_hi")
        xnT_lo = sem("xnT_lo")
        q_ps = sem("q_ps")
        q_hi = sem("q_hi")
        q_lo = sem("q_lo")
        s_ps = sem("s_ps")
        max_done = sem("max_done")
        shift_done = sem("shift_done")
        prob_ready = sem("prob_ready")
        pt_ps = sem("pt_ps")
        pt_sb = sem("pt_sb")
        o_ps = sem("o_ps")
        rsum_done = sem("rsum_done")
        att_done = sem("att_done")
        x1_done = sem("x1_done")
        stat2_done = sem("stat2_done")
        mv2_done = sem("mv2_done")
        ve2_done = sem("ve2_done")
        rstd2_done = sem("rstd2_done")
        xn2_ready = sem("xn2_ready")
        row_hi = sem("row_hi")
        row_lo = sem("row_lo")
        xn2T_ps = sem("xn2T_ps")
        xn2T_sb = sem("xn2T_sb")
        logit_ps = sem("logit_ps")
        logit_sb = sem("logit_sb")
        w_hi = sem("w_hi")
        w_scaled = sem("w_scaled")
        w_lo = sem("w_lo")
        route_done = sem("route_done")
        exp_ready = sem("exp_ready")
        pick_ready = sem("pick_ready")
        rank_ps = sem("rank_ps")
        rank_used = sem("rank_used")
        slots_ready = sem("slots_ready")
        rows_sent = [sem(f"rows_sent{i}") for i in range(GT)]
        zero_made = sem("zero_made")
        dump_sent = sem("dump_sent")
        final_done = sem("final_done")
        blk_ready = sem("blk_ready")
        pads_sent = sem("pads_sent")
        xbT_ps = sem("xbT_ps")
        xbT_sb = sem("xbT_sb")
        h_ps = sem("h_ps")
        h_act = sem("h_act")
        h_hi = sem("h_hi")
        h_lo = sem("h_lo")
        h_used = sem("h_used")
        y_sb = sem("y_sb")
        picked = sem("picked")
        part_done = sem("part_done")
        res_done = sem("res_done")
        w_in = [sem(f"w_in{i}") for i in range(2)]
        xb_in = [sem(f"xb_in{i}") for i in range(2)]
        y_out = [sem(f"y_out{i}") for i in range(2)]
        out_sent = [sem(f"out_sent{i}") for i in range(2)]
        pick_in = [sem(f"pick_in{i}") for i in range(4)]

        def some(count):
            return not isinstance(count, int) or count > 0

        def attention_steps(eng, step):
            for s in range(2 * UNROLL):
                step(s, s % UNROLL, None)
            with eng.Fori(2, NT // UNROLL) as i:
                for u in range(UNROLL):
                    step(i * UNROLL + u, u, i - 2 if u > 0 else None)
            for s in range(NT, NT + 2 * UNROLL):
                step(s, s % UNROLL, s // UNROLL - 2 if s % UNROLL > 0 else None)

        def live(t):
            return not isinstance(t, int) or 0 <= t < NT

        def late(t):
            return isinstance(t, int) and t >= NT - GT


        def batch_of(eng, t):
            return t // TB if isinstance(t, int) else eng.snap(t // TB)

        block = ctx.enter_context(nc.Block())

        @block.sync
        def _(sp):
            xr = x.rearrange("b (t p) d -> p (b t) d", p=P)
            n = NT // 4
            sp.dma_start(wk, wkT.rearrange("(k p) n -> p k n", p=P)).then_inc(kv_in, 16)
            sp.dma_start(cT, ctxT.rearrange("(k p) n -> p k n", p=P)).then_inc(kv_in, 16)
            sp.dma_start(X[:, 0:n, :], xr[:, 0:n, :]).then_inc(x_in[0], 16)
            sp.dma_start(wv, wvT.rearrange("(k p) n -> p k n", p=P)).then_inc(kv_in, 16)
            sp.dma_start(vb[0:LK, :], v_b.rearrange("(o d) -> o d", o=1).broadcast_to([LK, D])).then_inc(kv_in, 16)
            sp.dma_start(wq[:, :, :], wqT.rearrange("(k p) n -> p k n", p=P)).then_inc(wq_in, 16)
            for c in range(1, 4):
                sp.dma_start(X[:, c * n:(c + 1) * n, :], xr[:, c * n:(c + 1) * n, :]).then_inc(x_in[c], 16)
            w1r = w1.rearrange("e (k p) f -> p e k f", p=P)
            w2r = w2.rearrange("e (c f p) d -> p e c f d", p=P, c=2)

            def load_expert(e):
                if some(e * 16):
                    sp.wait_ge(w_in[0], e * 16)
                sp.dma_start(Wf[:, at(e * 4 + 2, 2), :], w1r[:, at(e), :, :].rearrange("p o k f -> p (o k) f")
                             ).then_inc(w_in[0], 16)
                if some(e * 16):
                    sp.wait_ge(w_in[1], e * 16)
                sp.dma_start(Wf[:, at(e * 4 + 4, 2), :].rearrange("p c (f d) -> p c f d", d=D),
                             w2r[:, at(e), :, :, :].rearrange("p o c f d -> p (o c) f d")).then_inc(w_in[1], 16)

            load_expert(0)
            with sp.Fori(1, E) as e:
                load_expert(e)

            sp.wait_ge(blk_ready, 1)
            sp.wait_ge(dump_sent, 16)
            r = sp.alloc_register("row")
            for e in range(E):
                sp.reg_load(r, padi[0:1, e:e + 1])
                sp.dma_start(xs[at(sp.snap(r, min_val=0, max_val=(E - 1) * CAP + B * L), MB), :].rearrange(
                    "(h p) d -> p h d", p=P), zrows).then_inc(pads_sent, 16)
            sp.wait_ge(pads_sent, 16 * E)
            sp.wait_ge(blk_ready, 3)
            for k in range(GT):
                sp.wait_ge(rows_sent[k], 32 * (NT // GT))

            def load_block(j, a):
                if some(j - 1):
                    n = sp.snap(j - 1)
                    sp.wait_ge(const_made, CONSTS)
                    sp.wait_ge(xbT_ps, n)
                sp.reg_load(r, blk[0:1, 1, at(j)])
                sp.dma_start(xb[:, a, :, :], xs[at(sp.snap(r, min_val=0, max_val=DUMP), MB), :].rearrange(
                    "(h p) d -> p h d", p=P)).then_inc(xb_in[a], 16)

            def store_block(j, a):
                n = sp.snap(j + 1)
                sp.wait_ge(const_made, CONSTS)
                sp.wait_ge(y_sb, n)
                sp.dma_start(ys[at(j * MB, MB), :].rearrange("(h p) d -> p h d", p=P), yb[:, a, :, :]).then_inc(y_out[a], 16)

            load_block(0, 0)
            load_block(1, 1)
            load_block(2, 0)
            with sp.Fori(0, (NB - 3) // 2) as i:
                for a in range(2):
                    load_block(i * 2 + a + 3, (a + 1) % 2)
                    store_block(i * 2 + a, a)
            for j in range(NB - 3, NB):
                store_block(j, j % 2)

            outr = out.rearrange("b (t p) d -> p (b t) d", p=P)
            with sp.Fori(0, NT // 2) as i:
                for a in range(2):
                    sp.wait_ge(res_done, i * 2 + a + 1)
                    sp.dma_start(outr[:, at(i * 2 + a), :].rearrange("p o d -> p (o d)"),
                                 res[:, a, :]).then_inc(out_sent[a], 16)
            for a in range(2):
                sp.wait_ge(out_sent[a], NT // 2 * 16)

        @block.gpsimd
        def _(pool):
            pool.memset(ident[:, :], 0.0).then_inc(const_made, 1)
            pool.memset(ident16[:, :], 0.0).then_inc(const_made, 1)
            pool.memset(neghalf[:, :], -0.5).then_inc(const_made, 1)
            pool.memset(ones[:, :], 1.0).then_inc(const_made, 1)
            pool.memset(wscale[:, :], WSCALE).then_inc(const_made, 1)
            pool.memset(before[:, :], 1.0).then_inc(const_made, 1)
            pool.memset(headm[:, :, :], 1.0).then_inc(const_made, 1)
            pool.memset(chunkm[:, :, :], 1.0).then_inc(const_made, 1)
            pool.memset(spread[0:LK, :], 0.0).then_inc(const_made, 1)
            pool.memset(vaug[0:LK, :, :, HD:VW], 1.0).then_inc(const_made, 1)
            pool.memset(count[:, :], 0.0).then_inc(const_made, 1)
            pool.wait_ge(const_made, CONSTS)
            for t in (ident, ident16):
                pool.affine_select(out=t[:, :], in_=t[:, :], compare_op=ALU.not_equal, fill=1.0, base=0,
                                   pattern=[[-1, P]], channel_multiplier=1).then_inc(ident_made, 1)
            pool.affine_select(out=headm[:, :, 0], in_=headm[:, :, 0], compare_op=ALU.is_ge, fill=0.0, base=0,
                               pattern=[[-HD, HG]], channel_multiplier=1).then_inc(head_made, 1)
            pool.wait_ge(head_made, 1)
            pool.affine_select(out=headm[:, :, 0], in_=headm[:, :, 0], compare_op=ALU.is_ge, fill=0.0, base=HD - 1,
                               pattern=[[HD, HG]], channel_multiplier=-1).then_inc(head_made, 1)
            for n in range(-(-(LK + P) // LK)):
                pool.affine_select(out=spread[0:LK, :], in_=spread[0:LK, :], compare_op=ALU.not_equal, fill=1.0,
                                   base=n * LK, pattern=[[-1, LK + P]], channel_multiplier=1).then_inc(chunk_made, 1)
                pool.wait_ge(chunk_made, n + 1)
            nsp = -(-(LK + P) // LK)
            for c in range(NC):
                pool.affine_select(out=chunkm[:, c, :], in_=chunkm[:, c, :], compare_op=ALU.is_ge, fill=0.0,
                                   base=c * P - LK * head0[c], pattern=[[-LK, CH]],
                                   channel_multiplier=1).then_inc(chunk_made, 1)
            pool.wait_ge(chunk_made, nsp + NC)
            for c in range(NC):
                pool.affine_select(out=chunkm[:, c, :], in_=chunkm[:, c, :], compare_op=ALU.is_ge, fill=0.0,
                                   base=LK * head0[c] + LK - 1 - c * P, pattern=[[LK, CH]],
                                   channel_multiplier=-1).then_inc(chunk_made, 1)
            pool.affine_select(out=before[:, :], in_=before[:, :], compare_op=ALU.is_gt, fill=0.0, base=0,
                               pattern=[[1, P]], channel_multiplier=-1).then_inc(chunk_made, 1)
            pool.iota(iota_i[:, 0, :], pattern=[[MB, NB]], base=0, channel_multiplier=0).then_inc(chunk_made, 1)
            pool.iota(iota_i[:, 1, :], pattern=[[1, NB]], base=0, channel_multiplier=0).then_inc(chunk_made, 1)
            pool.wait_ge(chunk_made, nsp + 2 * NC + 3)
            pool.tensor_copy(kstep[:, :], iota_i[:, 0, 0:NT]).then_inc(chunk_made, 1)
            pool.tensor_copy(jstep[:, :], iota_i[0:1, 1, :]).then_inc(chunk_made, 1)
            pool.tensor_scalar(desc[:, :], iota_i[:, 1, 0:E], -1.0, float(E), ALU.mult, ALU.add).then_inc(chunk_made, 1)
            pool.tensor_scalar(eoff[:, :], iota_i[:, 1, 0:E], float(CAP), None, ALU.mult).then_inc(chunk_made, 1)

            def inverse_deviation(c):
                q = slice(c * NT // 4, (c + 1) * NT // 4)
                pool.wait_ge(mv1_done, (c + 1) * NT // 4)
                pool.tensor_scalar(ve1[:, q], mv1[:, q, 1], EPS, None, ALU.add).then_inc(ve1_done, 1)
                pool.wait_ge(ve1_done, c + 1)
                pool.tensor_tensor(rstd1[:, q], ve1[:, q], neghalf[:, q], ALU.pow).then_inc(rstd1_done, 1)

            inverse_deviation(0)
            pool.wait_ge(kT_lo, 1)
            pool.wait_ge(head_made, 2)
            for g in range(NG):
                for h in range(2):
                    pool.tensor_tensor(
                        kbd[:, 1, g, h, :].rearrange("p (h k) -> p h k", h=HG),
                        kTs[:, h, g, LK:2 * LK].rearrange("p (o k) -> p o k", o=1).broadcast_to([P, HG, LK]),
                        headm[:, :, :].broadcast_to([P, HG, LK]), ALU.mult).then_inc(kbd_done, 1)
            def stand_in_rows():
                pool.wait_ge(w_lo, WCH)
                pool.memset(zrows, 0.0).then_inc(zero_made, 1)
                pool.memset(upto[:, :, :], 1.0).then_inc(zero_made, 1)
                pool.wait_ge(zero_made, 2)
                pool.affine_select(out=upto[:, :, :], in_=upto[:, :, :], compare_op=ALU.is_ge, fill=0.0, base=0,
                                   pattern=[[1, E], [-1, E]], channel_multiplier=0).then_inc(zero_made, 1)
                pool.dma_start(xs[DUMP:DUMP + MB, :].rearrange("(h p) d -> p h d", p=P), zrows).then_inc(dump_sent, 16)

            def scatter(k, slots, rows):
                for c in range(2):
                    pool.indirect_dma_start(
                        out=xs[:, :], out_offset=bass.IndirectOffsetOnAxis(ap=slots[:, c, k:k + 1], axis=0),
                        in_=rows[:, k, :], in_offset=None).then_inc(rows_sent[k], 16)

            def step(s, u, grp):
                last = isinstance(grp, int) and grp == NT // GT - 1
                group = (sloti_late, rows_late) if last else (sloti, rows)
                if isinstance(s, int) and s == NT + 2:
                    stand_in_rows()
                if grp is not None and u == 3:
                    t0 = s - (2 * UNROLL + 3)
                    pool.wait_ge(row_lo, t0 + GT)
                    pool.wait_ge(slots_ready, grp + 1)
                    pool.tensor_tensor(held[:, :], neghalf[:, 0:1], neghalf[:, 0:1], ALU.mult)
                    scatter(0, *group)
                    scatter(1, *group)
                t = s
                if live(t):
                    n = pool.snap(t + 1)
                    pool.wait_ge(const_made, CONSTS)
                    pool.wait_ge(w_scaled, n)
                    for c in (1, 0) if u in POOL_LOW else (1,):
                        pool.tensor_tensor(W[:, at(t * 2 + c), 1, :].rearrange("p o f -> p (o f)"),
                                           Wf[:, at(t * 2 + c + 2), :].rearrange("p o f -> p (o f)"),
                                           W[:, at(t * 2 + c), 0, :].rearrange("p o f -> p (o f)"),
                                           ALU.subtract).then_inc(w_lo, 1)
                if isinstance(s, int) and s == 1:
                    for c in range(1, 4):
                        inverse_deviation(c)
                t, a = s - 3, (u + 1) % 2
                if live(t):
                    pool.wait_ge(ve2_done, t + 1)
                    if some(t - 1):
                        pool.wait_ge(xn2_ready, t - 1)
                    pool.tensor_tensor(rstd2[:, a, :], ve2[:, a, :], neghalf[:, 0:1], ALU.pow).then_inc(rstd2_done, 1)
                t, r = s - 7, (u + 1) % GT
                if live(t) and not late(t):
                    pool.wait_ge(row_hi, t + 1)
                    pool.tensor_tensor(rows[:, r, D:2 * D], xn2[:, r, :], rows[:, r, 0:D],
                                       ALU.subtract).then_inc(row_lo, 1)
                if isinstance(s, int) and s == NT + 2 * UNROLL - 2:
                    for t in range(NT - GT, NT):
                        pool.wait_ge(row_hi, t + 1)
                        pool.tensor_tensor(rows_late[:, t % GT, D:2 * D], xn2[:, t % GT, :], rows_late[:, t % GT, 0:D],
                                           ALU.subtract).then_inc(row_lo, 1)
                if grp is not None and u == 3:
                    scatter(2, *group)
                    scatter(3, *group)

            attention_steps(pool, step)

            pool.wait_ge(final_done, 7)
            pool.wait_ge(pads_sent, 16 * E)
            for a in range(2):
                pool.wait_ge(y_out[a], 16 * ((NB + 1 - a) // 2))

            def gather(t, a):
                for c in range(2):
                    pool.indirect_dma_start(
                        out=picks[:, a, c, :], out_offset=None, in_=ys[:, :],
                        in_offset=bass.IndirectOffsetOnAxis(ap=csloti[:, c, t:t + 1], axis=0)).then_inc(pick_in[a], 16)

            for t in range(NT):
                if some(t - 3):
                    pool.wait_ge(res_done, t - 3)
                gather(t, t % 4)

        @block.scalar
        def _(act):
            act.dma_start(qb[:, :], q_b).then_inc(small_in, 16)
            act.dma_start(kb[:, :], k_b).then_inc(small_in, 16)
            act.dma_start(gains[:, 0:1], g_xattn.rearrange("(o d) -> o d", o=1).broadcast_to([P, 1])).then_inc(gains_in, 16)
            act.dma_start(gains[:, 1:2], g_ffn.rearrange("(o d) -> o d", o=1).broadcast_to([P, 1])).then_inc(gains_in, 16)
            act.dma_start(maski[:, :, :], mask.rearrange("(o b) k -> o b k", o=1)).then_inc(mask_in, 16)
            act.dma_start(gate[:, :, :], gate_w.rearrange("(k p) e -> p k e", p=P)).then_inc(gate_in, 16)
            act.wait_ge(gains_in, 32)
            act.activation(gains[:, 2:4], gains[:, 0:2], ACT.Tanh).then_inc(tanh_done, 1)
            act.wait_ge(small_in, 32)
            act.activation(qb16[:, :], qb[:, :], ACT.Copy, scale=QSCALE).then_inc(qb_done, 1)
            act.wait_ge(wq_in, 16)
            act.activation(wqs[:, 0, :, :], wq[:, :, :], ACT.Copy, scale=QSCALE).then_inc(wq_hi, 1)
            for g in range(NG):
                act.wait_ge(k_ps, 1)
                act.activation(kTf[:, g, :], pQ[:, g * B * LK:(g + 1) * B * LK], ACT.Identity,
                               bias=kb[:, g:g + 1]).then_inc(k_sb, 1)
            act.wait_ge(k_sb, NG)
            act.activation(kTs[:, 0, :, :], kTf[:, :, :], ACT.Copy).then_inc(kT_hi, 1)
            act.wait_ge(qb_done, 1)

            def step(s, u, grp):
                def probabilities_out(t, r):
                    act.wait_ge(pt_ps, t * 3 + r + 1)
                    if r == 0:
                        if some(t):
                            act.wait_ge(o_ps, t)
                    lo_c, hi_c = 4 * r, min(4 * r + 4, NC)
                    full = hi_c if hi_c < NC else NC - 1
                    last = act.activation(probT[:, lo_c * P:full * P], pP[:, r % 2, 0:(full - lo_c) * P], ACT.Copy)
                    if hi_c == NC:
                        last = act.activation(probT[0:TAIL, full * P:NC * P],
                                              pP[0:TAIL, r % 2, (full - lo_c) * P:(NC - lo_c) * P], ACT.Copy)
                    last.then_inc(pt_sb, 1)

                def weight_high(c):
                    act.activation(W[:, at(s * 2 + c), 0, :].rearrange("p o f -> p (o f)"),
                                   Wf[:, at(s * 2 + c + 2), :].rearrange("p o f -> p (o f)"),
                                   ACT.Copy, scale=WSCALE).then_inc(w_hi, 1)

                if live(s - 3):
                    probabilities_out(s - 3, 0)
                    probabilities_out(s - 3, 1)
                t, a = s - 5, (u + 1) % 2
                if live(t):
                    act.wait_ge(xn2T_ps, t + 1)
                    if some(t - 1):
                        act.wait_ge(logit_ps, t - 1)
                    act.activation(xn2T[:, a, :], pT[:, 0:D], ACT.Copy).then_inc(xn2T_sb, 1)
                if live(s - 3):
                    probabilities_out(s - 3, 2)
                t, a = s, u % 2
                if live(t):
                    act.wait_ge(xnT_ps, t + 1)
                    if some(t - 1):
                        act.wait_ge(q_ps, t - 1)
                    act.activation(xnT[:, a, 0, :, :], pT[:, 0:KD * P].rearrange("p (k n) -> p k n", k=KD),
                                   ACT.Copy).then_inc(xnT_hi, 1)
                if live(s):
                    act.wait_ge(w_in[u % 2], s * 8 + 16 - u % 2 * 8)
                    if some(s * 2):
                        n = act.snap(s * 2)
                        act.wait_ge(const_made, CONSTS)
                        act.wait_ge(w_lo, n)
                    weight_high(1)
                    weight_high(0)
                if grp is not None and u == 1:
                    act.wait_ge(route_done, grp * 26 + 2)
                    act.activation(rt["exp"][:, :, :], rt["shift"][:, :, :], ACT.Exp).then_inc(exp_ready, 1)
                t, a = s - 2, u % 2
                if live(t):
                    act.wait_ge(shift_done, t * 2 + 2)
                    act.activation(prob[:, a, :], prob[:, a, :], ACT.Exp,
                                   scale=float(HD) ** -0.5 / QSCALE).then_inc(prob_ready, 1)
                t, a = s, u % 2
                if live(t):
                    act.wait_ge(q_ps, t + 1)
                    if some(t - 1):
                        act.wait_ge(s_ps, t - 1)
                    for g in range(NG):
                        act.activation(qT[:, a, 0, g, :], pQ[:, g * P:(g + 1) * P], ACT.Identity,
                                       bias=qb16[:, g:g + 1]).then_inc(q_hi, 1)
                if live(s):
                    n = act.snap(s * 2 + 2)
                    act.wait_ge(const_made, CONSTS)
                    act.wait_ge(w_hi, n)
                    for c in (1, 0) if u in POOL_LOW else (1,):
                        last = act.activation(Wf[:, at(s * 2 + c + 2), :].rearrange("p o f -> p (o f)"),
                                              Wf[:, at(s * 2 + c + 2), :].rearrange("p o f -> p (o f)"),
                                              ACT.Copy, scale=WSCALE)
                    last.then_inc(w_scaled, 1)
                t, r = s - 7, (u + 1) % GT
                if live(t) and not late(t):
                    if some((t - r) * 8):
                        act.wait_ge(rows_sent[r], (t - r) * 8)
                    act.wait_ge(xn2_ready, t + 1)
                    act.activation(rows[:, r, 0:D], xn2[:, r, :], ACT.Copy).then_inc(row_hi, 1)
                if isinstance(s, int) and s == NT + 2 * UNROLL - 2:
                    for t in range(NT - GT, NT):
                        act.wait_ge(o_ps, NT)
                        act.wait_ge(xn2_ready, t + 1)
                        act.activation(rows_late[:, t % GT, 0:D], xn2[:, t % GT, :], ACT.Copy).then_inc(row_hi, 1)

            attention_steps(act, step)

            def gelu(j):
                for q in range(NQ):
                    act.wait_ge(h_ps, j * NQ + q + 1)
                    if some(j * NQ + q + 1 - NQ):
                        act.wait_ge(h_lo, j * NQ + q + 1 - NQ)
                    act.activation(hid[:, q, :], hbank[q][:, 0:512], ACT.Gelu_apprx_tanh,
                                   scale=1.0 / WSCALE).then_inc(h_act, 1)

            def y_copy(j, a, i):
                act.wait_ge(h_used, (j + 1) * NQ)
                if some(i * 16):
                    act.wait_ge(y_out[a], i * 16)
                act.activation(yb[:, a, :, :].rearrange("p h d -> p (h d)"), ybank[a], ACT.Copy).then_inc(y_sb, 1)

            gelu(0)
            gelu(1)
            y_copy(0, 0, 0)
            gelu(2)
            y_copy(1, 1, 0)
            with act.Fori(0, (NB - 3) // 2) as i:
                for u in range(2):
                    gelu(i * 2 + u + 3)
                    y_copy(i * 2 + u + 2, u % 2, i + u // 2 + 1)
            y_copy(NB - 1, (NB - 1) % 2, (NB - 1) // 2)

        @block.tensor
        def _(pe):
            pe.wait_ge(kv_in, 64)
            for g in range(NG):
                for k in range(KD):
                    mm = pe.matmul(pQ[:, g * B * LK:(g + 1) * B * LK], wk[:, k, g * P:(g + 1) * P], cT[:, k, :],
                                   start=(k == 0), stop=(k == KD - 1))
            mm.then_inc(k_ps, 1)
            for b in range(B):
                for k in range(KD):
                    mm = pe.matmul(pS[0:LK, b, 0:D], cT[:, k, b * LK:(b + 1) * LK], wv[:, k, :],
                                   start=(k == 0), stop=(k == KD - 1))
            mm.then_inc(v_ps, 1)
            pe.wait_ge(vaug_done, B)
            pe.wait_ge(chunk_made, -(-(LK + P) // LK))
            pe.wait_ge(const_made, CONSTS)
            for c in range(NC):
                r0 = P * c % LK
                o = c % (NC // 2) * B * CH * VW
                mm = pe.matmul(pP[:, c // (NC // 2), o:o + B * CH * VW].rearrange("p (b n) -> p b n", b=B),
                               spread[0:LK, r0:r0 + P],
                               vaug[0:LK, :, head0[c]:head0[c] + CH, :].rearrange("p b h w -> p b (h w)"),
                               start=True, stop=True)
            mm.then_inc(vc_ps, 1)
            pe.wait_ge(ident_made, 2)
            pe.wait_ge(wq_lo, 1)
            pe.wait_ge(k_sb, NG)

            def step(s, u, grp):
                tp, ap = s - 3, (u + 1) % 2

                def probabilities(r):
                    if some(tp * 3 + max(r - 1, 0)):
                        pe.wait_ge(pt_sb, tp * 3 + max(r - 1, 0))
                    for c in range(4 * r, min(4 * r + 4, NC)):
                        n = P if c < NC - 1 else TAIL
                        mm = pe.transpose(pP[0:n, r % 2, (c - 4 * r) * P:(c - 4 * r + 1) * P],
                                          prob[:, ap, c * P:c * P + n], ident[:, :])
                    mm.then_inc(pt_ps, 1)

                def values(r):
                    pe.wait_ge(pt_sb, tp * 3 + r + 1)
                    for c in range(4 * r, min(4 * r + 4, NC)):
                        n = P if c < NC - 1 else TAIL
                        mm = pe.matmul(pO[:, head0[c] * VW:(head0[c] + CH) * VW], probT[0:n, c * P:(c + 1) * P],
                                       vbd[0:n, at(b), c, :].rearrange("p o n -> p (o n)"),
                                       start=(c == 0), stop=(c == NC - 1), skip_group_check=True)
                    return mm

                if live(tp):
                    b = batch_of(pe, tp)
                    if isinstance(tp, int) and tp == 0:
                        pe.wait_ge(vbd_done, 2 * B)
                    pe.wait_ge(prob_ready, tp + 1)
                    probabilities(0)
                    probabilities(1)
                t, r = s - 5, (u - 5) % GT
                if live(t):
                    pe.wait_ge(xn2_ready, t + 1)
                    pe.wait_ge(xnT_lo, min(s, NT) if isinstance(s, int) else s)
                    if u == 3 and grp is not None:
                        pe.wait_ge(rank_used, grp + 1)
                    for k in range(KD):
                        mm = pe.transpose(pT[:, k * P:(k + 1) * P], xn2[:, r, k * P:(k + 1) * P], ident[:, :])
                    mm.then_inc(xn2T_ps, 1)
                if live(tp):
                    if some(tp):
                        pe.wait_ge(att_done, tp)
                    values(0)
                    probabilities(2)
                t, a = s, u % 2
                if live(t):
                    pe.wait_ge(xn_ready, t + 1)
                    if some(t - 4):
                        pe.wait_ge(xn2T_sb, t - 4)
                    if some(t):
                        pe.wait_ge(xnT_lo, t)
                    for k in range(KD):
                        mm = pe.transpose(pT[:, k * P:(k + 1) * P], xn[:, a, k * P:(k + 1) * P], ident[:, :])
                    mm.then_inc(xnT_ps, 1)
                if live(tp):
                    values(1)
                    values(2).then_inc(o_ps, 1)
                t, a = s, u % 2
                if live(t):
                    pe.wait_ge(xnT_lo, t + 1)
                    if some(NG * t):
                        pe.wait_ge(q_lo, NG * t)
                    for g in range(NG):
                        for n, (ws, k, xp) in enumerate([(ws, k, xp) for k in range(KD)
                                                         for ws, xp in ((0, 0), (0, 1), (1, 0))]):
                            mm = pe.matmul(pQ[:, g * P:(g + 1) * P], wqs[:, ws, k, g * P:(g + 1) * P],
                                           xnT[:, a, xp, k, :], start=(n == 0), stop=(n == 3 * KD - 1))
                    mm.then_inc(q_ps, 1)
                if grp is not None and u == 2:
                    pe.wait_ge(pick_ready, grp + 1)
                    pe.wait_ge(xn2T_sb, s - 4 if not isinstance(s, int) else min(s - 4, NT))
                    pe.wait_ge(xnT_lo, s + 1 if not isinstance(s, int) else min(s + 1, NT))
                    for k in range(GT + 1):
                        for m in range(min(k, GT)):
                            mm = pe.matmul(pT[:, k * E:(k + 1) * E], ones[:, :], pick16[:, m, :],
                                           start=(m == 0), stop=(k == GT and m == GT - 1))
                        if k < GT:
                            mm = pe.matmul(pT[:, k * E:(k + 1) * E], before[:, :], pick16[:, k, :],
                                           start=(k == 0), stop=True)
                    mm.then_inc(rank_ps, 1)
                t, a = s - 5, (u + 1) % 2
                if live(t):
                    pe.wait_ge(xn2T_sb, t + 1)
                    if isinstance(t, int) and t == 0:
                        pe.wait_ge(gate_in, 16)
                    pe.wait_ge(shift_done, 2 * min(s - 1, NT) if isinstance(s, int) else (s - 1) * 2)
                    if some(t):
                        pe.wait_ge(logit_sb, t)
                    for k in range(KD):
                        mm = pe.matmul(pS[:, 2, LG:LG + E], xn2T[:, a, k * P:(k + 1) * P], gate[:, k, :],
                                       start=(k == 0), stop=(k == KD - 1))
                    mm.then_inc(logit_ps, 1)
                t, a = s - 1, (u + 1) % 2
                if live(t):
                    b = batch_of(pe, t)
                    if isinstance(t, int) and t == 0:
                        pe.wait_ge(kbd_done, B * NG * 2)
                        pe.wait_ge(mask_done, 1)
                    pe.wait_ge(q_lo, NG * (t + 1))
                    if some(t * 2):
                        pe.wait_ge(shift_done, t * 2)
                    for bank, col, g, h0, nh in PARTS:
                        dst = pS[:, bank, col:col + nh * LK]
                        pe.matmul(dst, ones[0:1, :], maskrow[:, at(b), :, :].rearrange("p b o k -> p (b o) k").broadcast_to([1, nh, LK]),
                                  start=True, stop=False)
                        for qs, ks in ((0, 0), (0, 1), (1, 0)):
                            mm = pe.matmul(dst, qT[:, a, qs, g, :],
                                           kbd[:, at(b), g, ks, h0 * LK:(h0 + nh) * LK].rearrange("p o n -> p (o n)"),
                                           start=False, stop=(qs == 1))
                    mm.then_inc(s_ps, 1)

            attention_steps(pe, step)

            pe.wait_ge(blk_ready, 3)
            pe.wait_ge(w_lo, WCH)
            ereg = pe.alloc_register("block_expert")

            def load_x(j, a, i):
                pe.wait_ge(xb_in[a], (i + 1) * 16)
                if some(j - 1):
                    pe.wait_ge(xbT_sb, j - 1)
                for h in range(MH):
                    for n in range(2 * KD):
                        mm = pe.transpose(tbank[a].bitcast(F16)[:, n * MB + h * P:n * MB + (h + 1) * P],
                                          xb[:, a, h, n * P:(n + 1) * P], ident16[:, :])
                mm.then_inc(xbT_ps, 1)

            def up(j, a):
                pe.reg_load(ereg, blk[0:1, 0, at(j)])
                e = pe.snap(ereg, min_val=0, max_val=E - 1)
                pe.wait_ge(xbT_sb, j + 1)
                for q in range(NQ):
                    if some(j * NQ + q + 1 - NQ):
                        pe.wait_ge(h_act, j * NQ + q + 1 - NQ)
                    for f in range(QF * q, QF * (q + 1)):
                        dst = hbank[q][:, (f % QF) * MB:(f % QF + 1) * MB]
                        for n, (k, ws, xp) in enumerate([(k, ws, xp) for k in range(KD)
                                                         for ws, xp in ((0, 0), (0, 1), (1, 0))]):
                            mm = pe.matmul(dst, We[:, at(e), k, ws, f * P:(f + 1) * P].rearrange("p o n -> p (o n)"),
                                           xbT[:, a, xp, k, :], start=(n == 0), stop=(n == 3 * KD - 1))
                    mm.then_inc(h_ps, 1)

            def down(j, a):
                pe.reg_load(ereg, blk[0:1, 0, at(j)])
                e = pe.snap(ereg, min_val=0, max_val=E - 1)
                if some(j - 1):
                    pe.wait_ge(y_sb, j - 1)
                for q in range(NQ):
                    pe.wait_ge(h_lo, j * NQ + q + 1)
                    for f in range(QF * q, QF * (q + 1)):
                        for hp, ws in ((0, 0), (1, 0), (0, 1)):
                            for h in range(MH):
                                mm = pe.matmul(ybank[a][:, h * D:(h + 1) * D],
                                               hidS[:, q, hp, (f % QF) * MB + h * P:(f % QF) * MB + (h + 1) * P],
                                               We[:, at(e), 2 + f // (KF // 2), ws, f % (KF // 2) * D:(f % (KF // 2) + 1) * D
                                                  ].rearrange("p o n -> p (o n)"),
                                               start=(f + hp + ws + h == 0),
                                               stop=(f == KF - 1 and ws == 1 and h == MH - 1), skip_group_check=True)
                    mm.then_inc(h_used, 1)

            load_x(0, 0, 0)
            load_x(1, 1, 0)
            up(0, 0)
            load_x(2, 0, 1)
            up(1, 1)
            down(0, 0)
            with pe.Fori(0, (NB - 3) // 2) as i:
                for u in range(2):
                    j = i * 2 + u + 2
                    load_x(j + 1, (u + 1) % 2, i + (u + 3) // 2)
                    up(j, u % 2)
                    down(j - 1, (u + 1) % 2)
            up(NB - 1, (NB - 1) % 2)
            down(NB - 2, NB % 2)
            down(NB - 1, (NB - 1) % 2)

        @block.vector
        def _(dve):
            def statistics(c):
                dve.wait_ge(x_in[c], 16)
                for t in range(c * NT // 4, (c + 1) * NT // 4):
                    dve.bn_stats(stat1[:, t, :], X[:, t, :]).then_inc(stat1_done, 1)
                for t in range(c * NT // 4, (c + 1) * NT // 4):
                    dve.wait_ge(stat1_done, t + 1)
                    dve.bn_aggr(mv1[:, t, :], stat1[:, t, :]).then_inc(mv1_done, 1)

            statistics(0)
            dve.wait_ge(wq_hi, 1)
            dve.scalar_tensor_tensor(out=wqs[:, 1, :, :], in0=wq[:, :, :], scalar=QSCALE, in1=wqs[:, 0, :, :],
                                     op0=ALU.mult, op1=ALU.subtract).then_inc(wq_lo, 1)
            dve.wait_ge(kT_hi, 1)
            dve.tensor_tensor(kTs[:, 1, :, :], kTf[:, :, :], kTs[:, 0, :, :], ALU.subtract).then_inc(kT_lo, 1)
            dve.wait_ge(v_ps, 1)
            dve.wait_ge(const_made, CONSTS)
            for b in range(B):
                dve.tensor_tensor(vaug[0:LK, b, :, 0:HD], pS[0:LK, b, 0:D].rearrange("p (h w) -> p h w", h=H),
                                  vb[0:LK, :].rearrange("p (h w) -> p h w", h=H), ALU.add).then_inc(vaug_done, 1)
            dve.wait_ge(tanh_done, 1)
            dve.tensor_scalar(gffn[:, :], gains[:, 3:4], 1.0 / WSCALE, None, ALU.mult).then_inc(final_done, 1)
            dve.wait_ge(final_done, 1)
            dve.wait_ge(qb_done, 1)

            SELECT = 20

            def wide(v):
                return v.rearrange("p (t o) -> p t o", o=1).broadcast_to([P, GT, E])

            def shift_logits(g, t0):
                dve.wait_ge(logit_sb, t0 + GT)
                lg = logit[:, at(t0, GT), :]
                dve.tensor_reduce(rv["max"][:, :], lg, AX.X, ALU.max).then_inc(route_done, 1)
                dve.wait_ge(route_done, g * 26 + 1)
                dve.tensor_tensor(rt["shift"][:, :, :], lg, wide(rv["max"][:, :]), ALU.subtract).then_inc(route_done, 1)

            def select_experts(g, t0):
                R, V = rt, rv
                base = g * 26
                n = 2

                def done(ins):
                    nonlocal n
                    n += 1
                    ins.then_inc(route_done, 1)

                def after():
                    dve.wait_ge(route_done, base + n)

                dsc = desc[:, :].rearrange("p (o e) -> p o e", o=1).broadcast_to([P, GT, E])
                oh1 = chosen[:, 0, at(t0, GT), :]
                oh2 = chosen[:, 1, at(t0, GT), :]
                dve.wait_ge(exp_ready, g + 1)
                done(dve.tensor_reduce(V["sum"][:, :], R["exp"][:, :, :], AX.X, ALU.add))
                after()
                done(dve.reciprocal(V["rsum"][:, :], V["sum"][:, :]))
                after()
                done(dve.tensor_tensor(R["p"][:, :, :], R["exp"][:, :, :], wide(V["rsum"][:, :]), ALU.mult))
                after()
                done(dve.tensor_reduce(V["m1"][:, :], R["p"][:, :, :], AX.X, ALU.max))
                after()
                done(dve.tensor_tensor(R["eq"][:, :, :], R["p"][:, :, :], wide(V["m1"][:, :]), ALU.is_equal))
                after()
                done(dve.tensor_tensor(R["c"][:, :, :], R["eq"][:, :, :], dsc, ALU.mult))
                after()
                done(dve.tensor_reduce(V["f1"][:, :], R["c"][:, :, :], AX.X, ALU.max))
                after()
                done(dve.tensor_tensor(oh1, dsc, wide(V["f1"][:, :]), ALU.is_equal))
                after()
                done(dve.scalar_tensor_tensor(out=R["p2"][:, :, :], in0=oh1, scalar=-2.0, in1=R["p"][:, :, :],
                                              op0=ALU.mult, op1=ALU.add))
                after()
                done(dve.tensor_reduce(V["m2"][:, :], R["p2"][:, :, :], AX.X, ALU.max))
                after()
                done(dve.tensor_tensor(R["eq"][:, :, :], R["p2"][:, :, :], wide(V["m2"][:, :]), ALU.is_equal))
                after()
                done(dve.tensor_tensor(R["c"][:, :, :], R["eq"][:, :, :], dsc, ALU.mult))
                after()
                done(dve.tensor_reduce(V["f2"][:, :], R["c"][:, :, :], AX.X, ALU.max))
                after()
                done(dve.tensor_tensor(oh2, dsc, wide(V["f2"][:, :]), ALU.is_equal))
                after()
                dve.tensor_tensor(pick16[:, :, :], oh1, oh2, ALU.add).then_inc(pick_ready, 1)
                done(dve.tensor_tensor(V["ws"][:, :], V["m1"][:, :], V["m2"][:, :], ALU.add))
                after()
                done(dve.reciprocal(V["rws"][:, :], V["ws"][:, :]))
                after()
                for c, m in enumerate(("m1", "m2")):
                    done(dve.scalar_tensor_tensor(out=comb[:, c, at(t0, GT)], in0=V[m][:, :], scalar=gffn[:, 0:1],
                                                  in1=V["rws"][:, :], op0=ALU.mult, op1=ALU.mult))
                assert n == SELECT, n

            def give_slots(g, t0):
                R = rt
                base = g * 26
                n = SELECT
                oh1 = chosen[:, 0, at(t0, GT), :]
                oh2 = chosen[:, 1, at(t0, GT), :]

                def done(ins):
                    nonlocal n
                    n += 1
                    ins.then_inc(route_done, 1)

                def after():
                    dve.wait_ge(route_done, base + n)

                dve.wait_ge(rank_ps, g + 1)
                done(dve.tensor_tensor(R["rank"][:, :, :], pT[:, 0:GT * E].rearrange("p (t e) -> p t e", t=GT),
                                       count[:, :].rearrange("p (o e) -> p o e", o=1).broadcast_to([P, GT, E]), ALU.add))
                after()
                dve.tensor_tensor(count[:, :], pT[:, GT * E:(GT + 1) * E], count[:, :], ALU.add).then_inc(rank_used, 1)
                dve.wait_ge(rank_used, g + 1)
                done(dve.tensor_tensor(R["rank"][:, :, :], R["rank"][:, :, :],
                                       eoff[:, :].rearrange("p (o e) -> p o e", o=1).broadcast_to([P, GT, E]), ALU.add))
                after()
                done(dve.tensor_tensor(R["s1"][:, :, :], R["rank"][:, :, :], oh1, ALU.mult))
                done(dve.tensor_tensor(R["s2"][:, :, :], R["rank"][:, :, :], oh2, ALU.mult))
                after()
                done(dve.tensor_reduce(slot[:, 0, at(t0, GT)], R["s1"][:, :, :], AX.X, ALU.add))
                done(dve.tensor_reduce(slot[:, 1, at(t0, GT)], R["s2"][:, :, :], AX.X, ALU.add))
                after()
                last = isinstance(g, int) and g == NT // GT - 1
                if not last:
                    dve.wait_ge(row_hi, t0 + GT)
                dve.tensor_scalar((sloti_late if last else sloti)[:, :, :], slot[:, :, at(t0, GT)], 0.0, None, ALU.add).then_inc(slots_ready, 1)
                assert n == 26, n

            def normalise(t, a):
                if some(t - 1):
                    dve.wait_ge(xnT_ps, t - 1)
                dve.tensor_scalar(xn[:, a, :], X[:, at(t), :].rearrange("p o d -> p (o d)"),
                                  mv1[:, at(t), 0], rstd1[:, at(t)], ALU.subtract,
                                  ALU.mult).then_inc(xn_ready, 1)

            def block_diagonal_keys():
                dve.wait_ge(kT_lo, 1)
                dve.wait_ge(head_made, 2)
                for g in range(NG):
                    for h in range(2):
                        dve.tensor_tensor(
                            kbd[:, 0, g, h, :].rearrange("p (h k) -> p h k", h=HG),
                            kTs[:, h, g, 0:LK].rearrange("p (o k) -> p o k", o=1).broadcast_to([P, HG, LK]),
                            headm[:, :, :].broadcast_to([P, HG, LK]), ALU.mult).then_inc(kbd_done, 1)
                dve.wait_ge(mask_in, 16)
                dve.tensor_scalar(maskrow[:, :, 0, :], maski[:, :, :],
                                  0.0, MASKED, ALU.is_gt, ALU.mult).then_inc(mask_done, 1)

            def block_diagonal_values():
                dve.wait_ge(vc_ps, 1)
                dve.wait_ge(chunk_made, -(-(LK + P) // LK) + 2 * NC + 7)
                for b in range(B):
                    for n in range(2):
                        hc = NC // 2
                        src = pP[:, n, 0:hc * B * CH * VW].rearrange("p (c b h w) -> p b c h w", b=B, c=hc, h=CH)
                        dve.tensor_tensor(vbd[:, b, n * hc:(n + 1) * hc, :].rearrange("p c (h w) -> p c h w", h=CH),
                                          src[:, b, :, :, :],
                                          chunkm[:, n * hc:(n + 1) * hc, :].rearrange("p c (h o) -> p c h o", o=1).broadcast_to(
                                              [P, hc, CH, VW]), ALU.mult).then_inc(vbd_done, 1)

            def step(s, u, grp):
                if live(s) and u != 2:
                    dve.wait_ge(rstd1_done, 1 if isinstance(s, int) and s < NT // 4 else 4)
                    normalise(s, u % 2)
                t = s - 6
                if live(t):
                    dve.wait_ge(s_ps, min(s - 1, NT) if isinstance(s, int) else s - 1)
                    n = dve.snap(t + 1)
                    dve.wait_ge(const_made, CONSTS)
                    dve.wait_ge(logit_ps, n)
                    dve.tensor_copy(logit[:, at(t), :].rearrange("p o e -> p (o e)"), pS[:, 2, LG:LG + E]).then_inc(logit_sb, 1)
                if grp is not None and u == 3:
                    give_slots(grp, s - (2 * UNROLL + 3))
                if grp is not None and u == 1:
                    shift_logits(grp, s - (2 * UNROLL + 1))
                t, a = s - 2, u % 2
                if live(t):
                    dve.wait_ge(s_ps, t + 1)
                    nb2 = 2 * HB
                    dve.tensor_reduce(mx[:, a, 0:nb2].rearrange("p (b h) -> p b h", b=2),
                                      pS[:, 0:2, 0:HB * LK].rearrange("p b (h k) -> p b h k", h=HB),
                                      AX.X, ALU.max).then_inc(max_done, 1)
                    dve.tensor_reduce(mx[:, a, nb2:H], pS[:, 2, 0:(H - nb2) * LK].rearrange("p (h k) -> p h k", k=LK),
                                      AX.X, ALU.max).then_inc(max_done, 1)
                    dve.wait_ge(max_done, t * 2 + 2)
                    if some(t * 3 - 3):
                        dve.wait_ge(pt_ps, t * 3 - 3)
                    dve.tensor_tensor(prob[:, a, 0:nb2 * LK].rearrange("p (b h k) -> p b h k", b=2, h=HB),
                                      pS[:, 0:2, 0:HB * LK].rearrange("p b (h k) -> p b h k", h=HB),
                                      mx[:, a, 0:nb2].rearrange("p (b h o) -> p b h o", b=2, o=1).broadcast_to([P, 2, HB, LK]),
                                      ALU.subtract).then_inc(shift_done, 1)
                t, a = s, u % 2
                if live(t):
                    dve.wait_ge(xnT_hi, t + 1)
                    dve.tensor_tensor(xnT[:, a, 1, :, :], pT[:, 0:KD * P].rearrange("p (k n) -> p k n", k=KD),
                                      xnT[:, a, 0, :, :], ALU.subtract).then_inc(xnT_lo, 1)
                t, a = s - 2, u % 2
                if live(t):
                    dve.tensor_tensor(prob[:, a, nb2 * LK:HK].rearrange("p (h k) -> p h k", k=LK),
                                      pS[:, 2, 0:(H - nb2) * LK].rearrange("p (h k) -> p h k", k=LK),
                                      mx[:, a, nb2:H].rearrange("p (h o) -> p h o", o=1).broadcast_to([P, H - nb2, LK]),
                                      ALU.subtract).then_inc(shift_done, 1)
                t, a, r = s - 4, u % 2, u % GT
                if live(t):
                    dve.wait_ge(rstd2_done, t + 1)
                    if some(t - GT + 1):
                        dve.wait_ge(xn2T_ps, t - GT + 1)
                        dve.wait_ge(row_lo, t - GT + 1)
                    dve.tensor_scalar(xn2[:, r, :], X[:, at(t), :].rearrange("p o d -> p (o d)"), mv2[:, a, 0:1],
                                      rstd2[:, a, :], ALU.subtract, ALU.mult).then_inc(xn2_ready, 1)
                t, a = s - 3, (u + 1) % 2
                if live(t):
                    dve.wait_ge(o_ps, t + 1)
                    heads = pO[:, 0:H * VW].rearrange("p (h w) -> p h w", h=H)
                    dve.reciprocal(rsum[:, a, :], heads[:, :, HD]).then_inc(rsum_done, 1)
                    dve.wait_ge(rsum_done, t + 1)
                    dve.tensor_tensor(att[:, :].rearrange("p (h w) -> p h w", h=H), heads[:, :, 0:HD],
                                      rsum[:, a, :].rearrange("p (h o) -> p h o", o=1).broadcast_to([P, H, HD]),
                                      ALU.mult).then_inc(att_done, 1)
                    dve.wait_ge(att_done, t + 1)
                    dve.wait_ge(xn_ready, t + 1)
                    xt = X[:, at(t), :].rearrange("p o d -> p (o d)")
                    dve.scalar_tensor_tensor(out=xt, in0=att[:, :], scalar=gains[:, 2:3], in1=xt,
                                             op0=ALU.mult, op1=ALU.add).then_inc(x1_done, 1)
                    n = dve.snap(t + 1)
                    dve.wait_ge(const_made, CONSTS)
                    dve.wait_ge(x1_done, n)
                    dve.bn_stats(stat2[:, a, :], xt).then_inc(stat2_done, 1)
                    n = dve.snap(t + 1)
                    dve.wait_ge(const_made, CONSTS)
                    dve.wait_ge(stat2_done, n)
                    dve.bn_aggr(mv2[:, a, :], stat2[:, a, :]).then_inc(mv2_done, 1)
                    dve.wait_ge(mv2_done, t + 1)
                    dve.tensor_scalar(ve2[:, a, :], mv2[:, a, 1:2], EPS, None, ALU.add).then_inc(ve2_done, 1)
                t = s
                if live(t) and u not in POOL_LOW:
                    dve.wait_ge(w_hi, t * 2 + 2)
                    dve.scalar_tensor_tensor(out=W[:, at(t * 2), 1, :].rearrange("p o f -> p (o f)"),
                                             in0=Wf[:, at(t * 2 + 2), :].rearrange("p o f -> p (o f)"), scalar=WSCALE,
                                             in1=W[:, at(t * 2), 0, :].rearrange("p o f -> p (o f)"),
                                             op0=ALU.mult, op1=ALU.subtract).then_inc(w_lo, 1)
                if isinstance(s, int) and s == 0:
                    block_diagonal_keys()
                t, a = s, u % 2
                if live(t):
                    dve.wait_ge(q_hi, NG * (t + 1))
                    for g in range(NG):
                        dve.scalar_tensor_tensor(out=qT[:, a, 1, g, :], in0=pQ[:, g * P:(g + 1) * P],
                                                 scalar=qb16[:, g:g + 1], in1=qT[:, a, 0, g, :],
                                                 op0=ALU.add, op1=ALU.subtract).then_inc(q_lo, 1)
                if live(s) and u == 1:
                    normalise(s + 1, (u + 1) % 2)
                if isinstance(s, int) and s == 1:
                    block_diagonal_values()
                    for c in range(1, 4):
                        statistics(c)
                if grp is not None and u == 1:
                    select_experts(grp, s - (2 * UNROLL + 1))

            attention_steps(dve, step)

            nfin = 1

            def fin(ins):
                nonlocal nfin
                nfin += 1
                ins.then_inc(final_done, 1)
                dve.wait_ge(final_done, nfin)

            def blkdone(ins):
                ins.then_inc(blk_ready, 1)

            dve.wait_ge(w_lo, WCH)
            dve.wait_ge(zero_made, 3)
            fin(dve.tensor_tensor(over[:, :, :], count[:, :].rearrange("p (e o) -> p e o", o=1).broadcast_to([P, E, NT]),
                                  kstep[:, :].rearrange("p (o k) -> p o k", o=1).broadcast_to([P, E, NT]), ALU.is_gt))
            dve.tensor_tensor(padrow[:, :], count[0:1, :], eoff[0:1, :], ALU.add).then_inc(max_done, 1)
            dve.wait_ge(max_done, 2 * NT + 1)
            blkdone(dve.tensor_copy(padi[:, :], padrow[:, :]))
            fin(dve.tensor_reduce(nblk[:, :], over[:, :, :], AX.X, ALU.add))
            fin(dve.tensor_tensor(cum[:, :, :], nblk[:, :].rearrange("p (o e) -> p o e", o=1).broadcast_to([P, E, E]),
                                  upto[:, :, :], ALU.mult))
            fin(dve.tensor_reduce(end[:, :], cum[:, :, :], AX.X, ALU.add))
            j_wide = jstep[:, :].rearrange("p (j o) -> p j o", o=1).broadcast_to([1, NB, E])
            chain = 2 * NT + 1

            def link(ins):
                nonlocal chain
                chain += 1
                ins.then_inc(max_done, 1)
                dve.wait_ge(max_done, chain)

            link(dve.tensor_tensor(past[:, :, :], j_wide,
                                   end[0:1, :].rearrange("p (o e) -> p o e", o=1).broadcast_to([1, NB, E]), ALU.is_ge))
            link(dve.memset(coef[:, E - 1:E], float(DUMP)))
            link(dve.tensor_scalar(coef[:, 0:E - 1], nblk[0:1, 0:E - 1], -float(MB), float(CAP), ALU.mult, ALU.add))
            link(dve.tensor_reduce(bexp, past[:, :, 0:E - 1], AX.X, ALU.add))
            link(dve.tensor_tensor(pastc[:, :, :], past[:, :, :],
                                   coef[:, :].rearrange("p (o e) -> p o e", o=1).broadcast_to([1, NB, E]), ALU.mult))
            blkdone(dve.tensor_copy(blk[:, 0, :], bexp))
            link(dve.tensor_reduce(brow[:, 0, :], pastc[:, :, :], AX.X, ALU.add))
            link(dve.scalar_tensor_tensor(out=brow[:, 1, :], in0=jstep[:, :], scalar=float(MB), in1=brow[:, 0, :],
                                          op0=ALU.mult, op1=ALU.add))
            blkdone(dve.tensor_scalar(blk[:, 1, :], brow[:, 1, :], float(DUMP), None, ALU.min))
            link(dve.tensor_tensor(delta[:, 0, :], end[:, :], nblk[:, :], ALU.subtract))
            link(dve.scalar_tensor_tensor(out=delta[:, 1, :], in0=delta[:, 0, :], scalar=float(MB), in1=eoff[:, :],
                                          op0=ALU.mult, op1=ALU.subtract))
            for c in range(2):
                link(dve.tensor_tensor(cd[:, c, :, :], chosen[:, c, :, :],
                                       delta[:, 1, :].rearrange("p (o e) -> p o e", o=1).broadcast_to([P, NT, E]), ALU.mult))
            link(dve.tensor_reduce(cdr[:, :, :], cd[:, :, :, :], AX.X, ALU.add))
            fin(dve.tensor_tensor(cslot[:, :, :], cdr[:, :, :], slot[:, :, :], ALU.add))
            fin(dve.tensor_copy(csloti[:, :, :], cslot[:, :, :]))
            assert nfin == 7, nfin

            def xb_copy(j, a):
                dve.wait_ge(xbT_ps, j + 1)
                if some(j * NQ - NQ):
                    dve.wait_ge(h_ps, j * NQ - NQ)
                dve.tensor_copy(xbT[:, a, :, :, :].rearrange("p s k n -> p (s k n)"),
                                tbank[a].bitcast(F16)).then_inc(xbT_sb, 1)

            def split(j):
                for q in range(NQ):
                    dve.wait_ge(h_act, j * NQ + q + 1)
                    if some(j * NQ + q + 1 - NQ):
                        dve.wait_ge(h_used, j * NQ + q + 1 - NQ)
                    dve.tensor_copy(hidS[:, q, 0, :], hid[:, q, :]).then_inc(h_hi, 1)
                    dve.wait_ge(h_hi, j * NQ + q + 1)
                    dve.tensor_tensor(hidS[:, q, 1, :], hid[:, q, :], hidS[:, q, 0, :], ALU.subtract).then_inc(h_lo, 1)

            xb_copy(0, 0)
            xb_copy(1, 1)
            split(0)
            xb_copy(2, 0)
            split(1)
            with dve.Fori(0, (NB - 3) // 2) as i:
                for u in range(2):
                    xb_copy(i * 2 + u + 3, (u + 1) % 2)
                    split(i * 2 + u + 2)
            split(NB - 1)

            def combine(t, a, r, i):
                dve.wait_ge(pick_in[a], (i + 1) * 32)
                if some((i * 2 + a // 2) * 16):
                    dve.wait_ge(out_sent[r], (i * 2 + a // 2) * 16)
                xt = X[:, at(t), :].rearrange("p o d -> p (o d)")
                dve.scalar_tensor_tensor(out=part[:, r, :], in0=picks[:, a, 0, :], scalar=comb[:, 0, at(t)], in1=xt,
                                         op0=ALU.mult, op1=ALU.add).then_inc(part_done, 1)
                dve.wait_ge(part_done, t + 1)
                dve.scalar_tensor_tensor(out=res[:, r, :], in0=picks[:, a, 1, :], scalar=comb[:, 1, at(t)],
                                         in1=part[:, r, :], op0=ALU.mult, op1=ALU.add).then_inc(res_done, 1)

            for t in range(4):
                combine(t, t, t % 2, 0)
            with dve.Fori(1, NT // 4) as i:
                for a in range(4):
                    combine(i * 4 + a, a, a % 2, i)


def kernel(**inputs):
    import numpy as np
    import concourse.bacc as bacc
    from concourse.bass_utils import run_bass_kernel_spmd as run

    def laid(a):
        return np.ascontiguousarray(a)

    nc = bacc.Bacc("TRN2", target_bir_lowering=False, num_devices=1)
    ctx = np.asarray(inputs["ctx_1024"])
    given = {
        "x": laid(inputs["x"]),
        "ctxT": laid(ctx.reshape(-1, ctx.shape[-1]).T),
        "mask": laid(inputs["mask_BxS2_ik0"]),
        "g_xattn": laid(inputs["g_xattn"]),
        "g_ffn": laid(inputs["g_ffn"]),
        "wqT": laid(np.asarray(inputs["L0_xattn_q_w"]).T),
        "q_b": laid(np.asarray(inputs["L0_xattn_q_b"]).reshape(-1, P).T),
        "wkT": laid(np.asarray(inputs["L0_xattn_k_w"]).T),
        "k_b": laid(np.asarray(inputs["L0_xattn_k_b"]).reshape(-1, P).T),
        "wvT": laid(np.asarray(inputs["L0_xattn_v_w"]).T),
        "v_b": laid(inputs["L0_xattn_v_b"]),
        "gate_w": laid(inputs["L0_ffn_gate_w"]),
        "w1": laid(inputs["L0_ffn_w1"]),
        "w2": laid(inputs["L0_ffn_w2"]),
    }
    args = [nc.dram_tensor("in_" + n, a.shape, mybir.dt.from_np(a.dtype), kind="ExternalInput").ap()
            for n, a in given.items()]
    out = nc.dram_tensor("out_0", given["x"].shape, F32, kind="ExternalOutput").ap()
    flamingo_moe_block(nc, *args, out)
    r = run(nc, [{"in_" + n: a for n, a in given.items()}], core_ids=[0])
    return r.results[0]["out_0"]
```
